# Optimizing a Trainium2 kernel written in Bass

```python
import numpy as np
import jax
import jax.numpy as jnp

def _softmax(x, axis=-1):
    return jax.nn.softmax(x, axis=axis)
def _gelu(x):
    return jax.nn.gelu(x, approximate=True)
def _silu(x):
    return jax.nn.silu(x)
def _sigmoid(x):
    return jax.nn.sigmoid(x)
def _layernorm(x, axis=-1, eps=1e-5):
    m = jnp.mean(x, axis=axis, keepdims=True)
    v = jnp.var(x, axis=axis, keepdims=True)
    return (x - m) / jnp.sqrt(v + eps)
def _scatter_add(tgt, idx, src, axis=0):
    return tgt.at[idx].add(src)
def _segment_sum(src, seg, n):
    return jax.ops.segment_sum(src, seg, n)

kernel_name = 'mk_adj_resnorm_d1_adj_512_ba9077'

def setup_inputs(seed: int = 0):
    np.random.seed(seed)
    _w = jnp.asarray
    def _rec_inputs():
        import jax
        import jax.numpy as jnp
        _gk = jax.random.key(seed)
        x = 7.22e-05 + 1 * jax.random.normal(jax.random.fold_in(_gk, 1), (128, 64, 512), jnp.float32)
        _a = jax.random.bernoulli(jax.random.fold_in(_gk, 2), 0.125, (64, 64))
        _a = jnp.logical_or(_a, jnp.swapaxes(_a, -1, -2))
        _a = jnp.logical_or(_a, jnp.eye(64, dtype=bool))
        adj = _a.astype(jnp.int32)
        return x, adj
    x, adj = _rec_inputs()
    def _L0_gnn_setup():
        import jax, jax.numpy as jnp
        import numpy as np
        LEAKY_ALPHA = 0.01
        NEG_INF = -1000000000.0
        LN_EPS = 1e-05

        def _gat_heads(x, adj, W, a):
            O = W.shape[-1]
            Wh = jnp.einsum('bnf,hfo->bhno', x, W)
            f1 = jnp.einsum('bhno,ho->bhn', Wh, a[:, :O])
            f2 = jnp.einsum('bhno,ho->bhn', Wh, a[:, O:])
            e = f1[:, :, :, None] + f2[:, :, None, :]
            e = jnp.where(e > 0, e, LEAKY_ALPHA * e)
            e = jnp.where(adj[None, None] > 0, e, NEG_INF)
            attn = jax.nn.softmax(e, axis=-1)
            return jnp.einsum('bhnm,bhmo->bhno', attn, Wh)
        key = jax.random.key(seed)
        ks = jax.random.split(key, 10)
        B, N, F_in, F_hid, H, F_out, D_ff = (8, 2048, 512, 512, 4, 512, 512)
        s = 0.05
        return {'enc_inputs': jax.random.normal(ks[0], (B, N, F_in), jnp.float32), 'adj': jax.random.randint(ks[1], (N, N), 0, 2, jnp.int32), 'W_heads': jax.random.normal(ks[2], (H, F_in, F_hid), jnp.float32) * s, 'a_heads': jax.random.normal(ks[3], (H, 2 * F_hid), jnp.float32) * s, 'W_out': jax.random.normal(ks[4], (H * F_hid, F_out), jnp.float32) * s, 'a_out': jax.random.normal(ks[5], (2 * F_out,), jnp.float32) * s, 'w1': jax.random.normal(ks[6], (F_out, D_ff), jnp.float32) * s, 'b1': jnp.zeros((D_ff,), jnp.float32), 'w2': jax.random.normal(ks[7], (D_ff, F_out), jnp.float32) * s, 'b2': jnp.zeros((F_out,), jnp.float32), 'ln_gamma': jnp.ones((F_out,), jnp.float32), 'ln_beta': jnp.zeros((F_out,), jnp.float32)}
    _L0_gnn_all = _L0_gnn_setup()
    _L0_gnn_in = {k: v for k, v in _L0_gnn_all.items() if k in ('W_heads', 'a_heads', 'W_out', 'a_out', 'w1', 'b1', 'w2', 'b2', 'ln_gamma', 'ln_beta', )}
    del _L0_gnn_all

    return {
        "x": x,
        "adj": adj,
        "L0_gnn_W_heads": _L0_gnn_in["W_heads"],
        "L0_gnn_a_heads": _L0_gnn_in["a_heads"],
        "L0_gnn_W_out": _L0_gnn_in["W_out"],
        "L0_gnn_a_out": _L0_gnn_in["a_out"],
        "L0_gnn_w1": _L0_gnn_in["w1"],
        "L0_gnn_b1": _L0_gnn_in["b1"],
        "L0_gnn_w2": _L0_gnn_in["w2"],
        "L0_gnn_b2": _L0_gnn_in["b2"],
        "L0_gnn_ln_gamma": _L0_gnn_in["ln_gamma"],
        "L0_gnn_ln_beta": _L0_gnn_in["ln_beta"],
    }

def reference(x, adj, L0_gnn_W_heads, L0_gnn_a_heads, L0_gnn_W_out, L0_gnn_a_out, L0_gnn_w1, L0_gnn_b1, L0_gnn_w2, L0_gnn_b2, L0_gnn_ln_gamma, L0_gnn_ln_beta):
    import jax
    import jax.numpy as jnp
    def _L0_gnn_ref(enc_inputs, adj, W_heads, a_heads, W_out, a_out, w1, b1, w2, b2, ln_gamma, ln_beta):
        import jax, jax.numpy as jnp
        import numpy as np
        LEAKY_ALPHA = 0.01
        NEG_INF = -1000000000.0
        LN_EPS = 1e-05

        def _gat_heads(x, adj, W, a):
            O = W.shape[-1]
            Wh = jnp.einsum('bnf,hfo->bhno', x, W)
            f1 = jnp.einsum('bhno,ho->bhn', Wh, a[:, :O])
            f2 = jnp.einsum('bhno,ho->bhn', Wh, a[:, O:])
            e = f1[:, :, :, None] + f2[:, :, None, :]
            e = jnp.where(e > 0, e, LEAKY_ALPHA * e)
            e = jnp.where(adj[None, None] > 0, e, NEG_INF)
            attn = jax.nn.softmax(e, axis=-1)
            return jnp.einsum('bhnm,bhmo->bhno', attn, Wh)
        B, N, _ = enc_inputs.shape
        h = jax.nn.elu(_gat_heads(enc_inputs, adj, W_heads, a_heads))
        h = jnp.transpose(h, (0, 2, 1, 3)).reshape(B, N, -1)
        out = _gat_heads(h, adj, W_out[None], a_out[None])[:, 0]
        out = jax.nn.elu(out)
        ffn = jnp.maximum(out @ w1 + b1, 0.0) @ w2 + b2
        y = ffn + out
        mu = jnp.mean(y, axis=-1, keepdims=True)
        var = jnp.var(y, axis=-1, keepdims=True)
        return (y - mu) / jnp.sqrt(var + LN_EPS) * ln_gamma + ln_beta

    x = _layernorm(x + _L0_gnn_ref(x, adj, L0_gnn_W_heads, L0_gnn_a_heads, L0_gnn_W_out, L0_gnn_a_out, L0_gnn_w1, L0_gnn_b1, L0_gnn_w2, L0_gnn_b2, L0_gnn_ln_gamma, L0_gnn_ln_beta), axis=-1)
    return x


_drawn_inputs = setup_inputs


def setup_inputs(seed=0):
    import zlib

    import numpy as np

    out = dict(_drawn_inputs(seed))
    spreads = {'L0_gnn_b1': (0.0, 0.1),
     'L0_gnn_b2': (0.0, 0.1),
     'L0_gnn_ln_gamma': (1.0, 0.2),
     'L0_gnn_ln_beta': (0.0, 0.1)}
    factors = {}
    for name, (base, spread) in spreads.items():
        noise = np.random.default_rng([zlib.crc32(name.encode()), seed]).standard_normal(out[name].shape)
        drawn = base * np.exp(spread * noise) if base else spread * noise
        out[name] = jnp.asarray(drawn.astype(out[name].dtype))
    for name, factor in factors.items():
        out[name] = (out[name] * factor).astype(out[name].dtype)
    return out
```

```python
from contextlib import ExitStack

import numpy as np


def build(nc, x, x_t, adj, w_heads, a_heads, w_out, a_out, w1, b1, w2, b2, gamma, beta, mid, out):
    layers_block(nc, x, x_t, adj, w_heads, a_heads, w_out, a_out, mid)
    ffn_block(nc, x, w1, b1, w2, b2, gamma, beta, mid, out)


def layers_block(nc, x, x_t, adj, w_heads, a_heads, w_out, a_out, mid):
    import concourse.bass as bass
    from concourse import mybir

    F32, F32R = mybir.dt.float32, mybir.dt.float32r
    ALU, ACT = mybir.AluOpType, mybir.ActivationFunctionType
    AX = mybir.AxisListType.X

    P = 128
    N = adj.shape[0]
    NH, F, O = w_heads.shape
    FT = F // P
    OT = O // P
    CB = 4
    CP = CB // 2
    T = CB * N
    CHUNKS = x.shape[0] // T
    TILES = NH * OT
    GQ = FT * CP
    LAG = 3
    RING = LAG + 1
    ALPHA = 0.01
    MASKED, OPEN = -1.0e9, 3.0e38
    assert 2 * N == P and T == 256 and F == 512 and O == 512 and CHUNKS % 2 == 0 and CHUNKS > 4

    with ExitStack() as ctx:
        def sb(name, shape, dt=F32):
            return ctx.enter_context(nc.sbuf_tensor(name, shape, dt))

        def sem(name):
            return ctx.enter_context(nc.semaphore(name))

        wh_hi = sb("wh_hi", [P, NH, FT, O], F32R)
        wh_lo = sb("wh_lo", [P, NH, FT, O], F32R)
        wo_hi = sb("wo_hi", [P, TILES, O], F32R)
        wo_lo = sb("wo_lo", [P, TILES, O], F32R)
        u = sb("u", [P, FT, 2 * NH])
        a_row = sb("a_row", [P, 2, O])
        x_dup = sb("x_dup", [P, F])
        x_split = sb("x_split", [P, CB, F], F32R)
        attn = sb("attn", [P, CP, NH, 2, N])
        attn_t_hi = sb("attn_t_hi", [P, CP, NH, P], F32R)
        attn_t_lo = sb("attn_t_lo", [P, CP, NH, P], F32R)
        g_hi = sb("g_hi", [P, NH, FT, T], F32R)
        g_lo = sb("g_lo", [P, NH, FT, T], F32R)
        h_full = sb("h_full", [P, 2, T])
        h_hi = sb("h_hi", [P, RING, T], F32R)
        h_lo = sb("h_lo", [P, RING, T], F32R)
        logits = sb("logits", [P, CP, 2 * NH])
        logits2 = sb("logits2", [P, 2, CP])
        attn2 = sb("attn2", [P, CP, N])
        attn2_bd = sb("attn2_bd", [P, CP, P])
        attn2_t_hi = sb("attn2_t_hi", [P, CP, P], F32R)
        attn2_t_lo = sb("attn2_t_lo", [P, CP, P], F32R)
        t_hi = sb("t_hi", [P, O], F32R)
        t_lo = sb("t_lo", [P, O], F32R)
        o_buf = sb("o_buf", [P, O])
        row_max = sb("row_max", [P, CP * NH])
        row_sum = sb("row_sum", [P, CP * NH])
        row_inv = sb("row_inv", [P, CP * NH])
        row_max2 = sb("row_max2", [P, CP])
        row_sum2 = sb("row_sum2", [P, CP])
        row_inv2 = sb("row_inv2", [P, CP])
        ident = sb("ident", [P, P])
        same_batch = sb("same_batch", [P, P])
        node_ident = sb("node_ident", [P, N])
        adj_i = sb("adj_i", [P, N], mybir.dt.int32)
        limit = sb("limit", [P, N])

        def bank(name):
            return ctx.enter_context(nc.psum_tensor(name, [P, 512], F32))

        t_ps = [[bank(f"t_ps{k}{p}") for p in range(CP)] for k in range(2)]
        h_ps = [bank(f"h_ps{k}") for k in range(2)]
        x_ps = [bank(f"x_ps{k}") for k in range(2)]

        adj_in, a_row_in, stage_in = sem("adj_in"), sem("a_row_in"), [sem(f"stage_in{k}") for k in range(4)]
        x_in, x_t_in, mid_out = sem("x_in"), sem("x_t_in"), sem("mid_out")
        const_step, const_done, limit_done = sem("const_step"), sem("const_done"), sem("limit_done")
        stage_hi, stage_lo, u_done = sem("stage_hi"), sem("stage_lo"), sem("u_done")
        x_hi_done, x_lo_done = sem("x_hi_done"), sem("x_lo_done")
        logits_ps, logits_sb = sem("logits_ps"), sem("logits_sb")
        diag_done, spread_ps, scores_done, exps_done = (
            sem("diag_done"), sem("spread_ps"), sem("scores_done"), sem("exps_done"))
        attn_done, attn_t_ps, attn_t_hi_done, attn_t_lo_done = (
            sem("attn_done"), sem("attn_t_ps"), sem("attn_t_hi_done"), sem("attn_t_lo_done"))
        front_step = sem("front_step")
        g_ps, g_hi_done, g_lo_done = sem("g_ps"), sem("g_hi_done"), sem("g_lo_done")
        h_ps_done, h_exp, h_min, h_elu, h_hi_done, h_lo_done, t_done = (
            sem("h_ps_done"), sem("h_exp"), sem("h_min"), sem("h_elu"), sem("h_hi_done"), sem("h_lo_done"),
            sem("t_done"))
        logits2_done, diag2_done, spread2_ps, scores2_done, exps2_done, attn2_done = (
            sem("logits2_done"), sem("diag2_done"), sem("spread2_ps"), sem("scores2_done"), sem("exps2_done"),
            sem("attn2_done"))
        attn2_t_ps, attn2_t_hi_done, attn2_t_lo_done = (
            sem("attn2_t_ps"), sem("attn2_t_hi_done"), sem("attn2_t_lo_done"))
        t_hi_done, t_lo_done, o_ps, o_exp, o_min, o_elu = (
            sem("t_hi_done"), sem("t_lo_done"), sem("o_ps"), sem("o_exp"), sem("o_min"), sem("o_elu"))
        tail_step = sem("tail_step")

        block = ctx.enter_context(nc.Block())

        attn_flat = attn[:, :, :, :, :].rearrange("p a h d n -> p (a h d n)")
        attn_g = attn[:, :, :, :, :].rearrange("p a h d n -> p (a h) d n")
        scores_g, attn_copy = attn_g[:, :, 0, :], attn_g[:, :, 1, :]
        stage = [attn_flat[:, 0:F], o_buf[:, :], h_full[:, :, :].rearrange("p a t -> p (a t)"),
                 attn_flat[:, F:2 * F]]
        tiles = [(w_heads[h, ft * P:(ft + 1) * P, :], wh_hi[:, h, ft, :], wh_lo[:, h, ft, :])
                 for h in range(NH) for ft in range(FT)]
        tiles += [(w_out[k * P:(k + 1) * P, :], wo_hi[:, k, :], wo_lo[:, k, :]) for k in range(TILES)]
        HEAD_TILES = NH * FT

        def after(eng, what, count):
            if not isinstance(count, int) or count > 0:
                eng.wait_ge(what, count)

        def chunks(eng, iteration):
            iteration(0, 0, first=True, last=False)
            iteration(1, 1, first=False, last=False)
            with eng.Fori(1, CHUNKS // 2 - 1, 1) as i:
                iteration(i * 2, 0, first=False, last=False)
                iteration(i * 2 + 1, 1, first=False, last=False)
            iteration(CHUNKS - 2, 0, first=False, last=False)
            iteration(CHUNKS - 1, 1, first=False, last=True)

        @block.sync
        def _(sp):
            for half in range(2):
                sp.dma_start(adj_i[half * N:(half + 1) * N, :], adj).then_inc(adj_in, 16)
            for i, (source, _, _) in enumerate(tiles):
                if i < HEAD_TILES and i % FT == 0:
                    h = i // FT
                    after(sp, u_done, 2 * FT * h)
                    sp.dma_start(a_row[:, :, :].rearrange("p a o -> p (a o)"),
                                 a_heads[h:h + 1, :].partition_broadcast(P)).then_inc(a_row_in, 16)
                if i >= 4:
                    sp.wait_ge(stage_lo, i - 3)
                    if i - 4 < HEAD_TILES:
                        sp.wait_ge(u_done, 2 * (i - 3))
                sp.dma_start(stage[i % 4], source).then_inc(stage_in[i % 4], 16)
            sp.wait_ge(u_done, 2 * HEAD_TILES)
            sp.dma_start(a_row[:, :, :].rearrange("p a o -> p (a o)"),
                         a_out[0:1, :].partition_broadcast(P)).then_inc(a_row_in, 16)
            sp.wait_ge(stage_lo, len(tiles))

            def load_x(c, b):
                after(sp, x_lo_done, c * CB + b)
                for half in range(2):
                    sp.dma_start(x_dup[half * N:(half + 1) * N, :],
                                 x[bass.ts(c * CB + b, N), :]).then_inc(x_in, 16)

            def load_x_t(c, p):
                if p == 0:
                    after(sp, attn_t_ps, c * CP)
                sp.dma_start(attn_flat[:, p * F:(p + 1) * F], x_t[bass.ts(c * CP + p, P), :])\
                    .then_inc(x_t_in, 16)

            def front(c):
                for p in range(CP):
                    load_x_t(c, p)
                for b in range(CB):
                    load_x(c, b)

            def tail(c):
                for p in range(CP):
                    sp.wait_ge(o_elu, c * CP + p + 1)
                    sp.dma_start(mid[bass.ts(c * CP + p, P), :], o_buf[:, :]).then_inc(mid_out, 16)

            def iteration(c, par, first, last):
                if not last:
                    front(c + 1)
                if not first:
                    tail(c - 1)

            front(0)
            chunks(sp, iteration)
            tail(CHUNKS - 1)
            sp.wait_ge(mid_out, 16 * CP * CHUNKS)

        @block.tensor
        def _(pe):
            mm, transpose = nc.tensor.matmul, nc.tensor.transpose

            def logits_of(c, p):
                if p == 0:
                    pe.wait_ge(x_t_in, (c + 1) * CP * 16)
                    after(pe, g_lo_done, c * GQ - 1)
                else:
                    pe.wait_ge(logits_sb, c * CP + p)
                for ft in range(FT):
                    last = mm(x_ps[0][:, 0:2 * NH], attn_flat[:, p * F + ft * P:p * F + (ft + 1) * P], u[:, ft, :],
                              start=ft == 0, stop=ft == FT - 1)
                last.then_inc(logits_ps, 1)

            def spread(c):
                pe.wait_ge(diag_done, c + 1)
                pe.wait_ge(logits_sb, c * CP + CP)
                mm(x_ps[0][:, :], same_batch[:, :], scores_g, start=True, stop=True).then_inc(spread_ps, 1)

            def transpose_attn(c, p):
                if p == 0:
                    pe.wait_ge(attn_done, c + 1)
                else:
                    pe.wait_ge(attn_t_lo_done, c * CP + p)
                for h in range(NH):
                    twice = attn[:, p, h, :, :].rearrange("p d n -> p (d n)")
                    last = transpose(x_ps[0][:, h * P:(h + 1) * P], twice, ident[:, :])
                last.then_inc(attn_t_ps, 1)

            def gather(c, q):
                ft, p = q // CP, q % CP
                if q == 0:
                    pe.wait_ge(attn_t_lo_done, c * CP + CP)
                    pe.wait_ge(x_lo_done, (c + 1) * CB)
                elif q == 1:
                    after(pe, o_elu, (c - 1) * CP)
                else:
                    pe.wait_ge(g_lo_done, c * GQ + q - 1)
                for b in range(2):
                    to = x_ps[q % 2][:, b * T:(b + 1) * T]
                    xb = x_split[:, 2 * p + b, ft * P:(ft + 1) * P]
                    mm(to, xb, attn_t_hi[:, p, :, b * N:(b + 1) * N], start=True, stop=False)
                    last = mm(to, xb, attn_t_lo[:, p, :, b * N:(b + 1) * N], start=False, stop=True)
                last.then_inc(g_ps, 1)

            def head(c, v):
                h, ot = v // OT, v % OT
                after(pe, h_elu, c * TILES + v - 1)
                to = h_ps[v % 2][:, 0:T]
                for ft in range(FT):
                    if v == 0:
                        pe.wait_ge(g_lo_done, c * GQ + (ft + 1) * CP)
                    w_hi = wh_hi[:, h, ft, ot * P:(ot + 1) * P]
                    w_lo = wh_lo[:, h, ft, ot * P:(ot + 1) * P]
                    mm(to, w_hi, g_hi[:, h, ft, :], start=ft == 0, stop=False)
                    mm(to, w_hi, g_lo[:, h, ft, :], start=False, stop=False)
                    last = mm(to, w_lo, g_hi[:, h, ft, :], start=False, stop=ft == FT - 1)
                last.then_inc(h_ps_done, 1)

            def add_out(c, par, v):
                pe.wait_ge(h_lo_done, c * TILES + v + 1)
                if v == 0:
                    after(pe, t_lo_done, (c - 1) * CP)
                for p in range(CP):
                    hh, hl = (s[:, v % RING, p * P:(p + 1) * P] for s in (h_hi, h_lo))
                    to = t_ps[par][p][:, :]
                    mm(to, hh, wo_hi[:, v, :], start=v == 0, stop=False)
                    mm(to, hh, wo_lo[:, v, :], start=False, stop=False)
                    last = mm(to, hl, wo_hi[:, v, :], start=False, stop=v == TILES - 1)
                last.then_inc(t_done, 1)

            def spread2(c, in_loop):
                pe.wait_ge(diag2_done, c + 1)
                if in_loop:
                    pe.wait_ge(g_lo_done, (c + 2) * GQ)
                else:
                    after(pe, o_elu, c * CP)
                mm(x_ps[1][:, 0:P], same_batch[:, :], attn2[:, :, :], start=True, stop=True)\
                    .then_inc(spread2_ps, 1)

            def transpose_attn2(c):
                pe.wait_ge(attn2_done, c + 1)
                for p in range(CP):
                    last = transpose(x_ps[1][:, p * P:(p + 1) * P], attn2_bd[:, p, :], ident[:, :])
                last.then_inc(attn2_t_ps, 1)

            def attend2(c, p):
                pe.wait_ge(t_lo_done, c * CP + p + 1)
                if p == 0:
                    pe.wait_ge(attn2_t_lo_done, c + 1)
                else:
                    pe.wait_ge(o_elu, c * CP + p)
                to = x_ps[1][:, :]
                mm(to, attn2_t_hi[:, p, :], t_hi[:, :], start=True, stop=False)
                mm(to, attn2_t_hi[:, p, :], t_lo[:, :], start=False, stop=False)
                mm(to, attn2_t_lo[:, p, :], t_hi[:, :], start=False, stop=True).then_inc(o_ps, 1)

            def iteration(c, par, first, last):
                for q in range(GQ):
                    gather(c, q)
                    if q in (1, 3, 5) and not first:
                        add_out(c - 1, 1 - par, TILES - LAG + q // 2)
                for v in range(TILES):
                    head(c, v)
                    if v >= LAG:
                        add_out(c, par, v - LAG)
                    if not first:
                        if v == 1:
                            spread2(c - 1, True)
                        if v == 5:
                            transpose_attn2(c - 1)
                        if v == 7:
                            attend2(c - 1, 0)
                        if v == 9:
                            attend2(c - 1, 1)
                    if not last:
                        if v == 1:
                            logits_of(c + 1, 0)
                        if v == 3:
                            logits_of(c + 1, 1)
                        if v == 6:
                            spread(c + 1)
                        if v == 11:
                            transpose_attn(c + 1, 0)
                        if v == 13:
                            transpose_attn(c + 1, 1)

            pe.wait_ge(u_done, 2 * HEAD_TILES)
            pe.wait_ge(const_done, 1)
            logits_of(0, 0)
            logits_of(0, 1)
            spread(0)
            transpose_attn(0, 0)
            transpose_attn(0, 1)
            pe.wait_ge(stage_lo, len(tiles))
            chunks(pe, iteration)
            for v in range(TILES - LAG, TILES):
                add_out(CHUNKS - 1, (CHUNKS - 1) % 2, v)
            spread2(CHUNKS - 1, False)
            transpose_attn2(CHUNKS - 1)
            attend2(CHUNKS - 1, 0)
            attend2(CHUNKS - 1, 1)

        @block.scalar
        def _(act):
            copy, exp = ACT.Copy, ACT.Exp

            def g_round(c, q):
                ft, p = q // CP, q % CP
                if q == 0:
                    after(act, h_ps_done, c * TILES)
                act.wait_ge(g_ps, c * GQ + q + 1)
                to = g_hi[:, :, ft, p * P:(p + 1) * P].rearrange("p h (b n) -> p b h n", b=2)
                act.activation(to, x_ps[q % 2][:, :].rearrange("p (b h n) -> p b h n", b=2, h=NH), copy)\
                    .then_inc(g_hi_done, 1)

            def x_round(c, b):
                act.wait_ge(x_in, (c * CB + b + 1) * 32)
                if b == 0:
                    after(act, g_ps, c * GQ)
                act.activation(x_split[:, b, :], x_dup[:, :], copy).then_inc(x_hi_done, 1)

            def exps(c):
                act.wait_ge(scores_done, c + 1)
                act.activation(scores_g, scores_g, exp).then_inc(exps_done, 1)

            def attn_t_round(c, p):
                act.wait_ge(attn_t_ps, c * CP + p + 1)
                after(act, g_ps, c * GQ)
                act.activation(attn_t_hi[:, p, :, :].rearrange("p h n -> p (h n)"), x_ps[0][:, :], copy)\
                    .then_inc(attn_t_hi_done, 1)

            def exps2(c):
                act.wait_ge(scores2_done, c + 1)
                act.activation(attn2[:, :, :], attn2[:, :, :], exp).then_inc(exps2_done, 1)

            def attn2_t_round(c):
                act.wait_ge(attn2_t_ps, c + 1)
                after(act, o_ps, c * CP)
                act.activation(attn2_t_hi[:, :, :].rearrange("p a n -> p (a n)"), x_ps[1][:, 0:CP * P], copy)\
                    .then_inc(attn2_t_hi_done, 1)

            def t_round(c, par, p):
                if p == 0:
                    act.wait_ge(t_done, (c + 1) * TILES)
                after(act, o_ps, c * CP + p)
                act.activation(t_hi[:, :], t_ps[par][p][:, :], copy).then_inc(t_hi_done, 1)

            def out_exp(c, p):
                act.wait_ge(o_ps, c * CP + p + 1)
                act.wait_ge(logits2_done, c + 1)
                after(act, mid_out, (c * CP + p) * 16)
                act.activation(o_buf[:, :], x_ps[1][:, :], exp).then_inc(o_exp, 1)

            def iteration(c, par, first, last):
                for q in range(GQ):
                    g_round(c, q)
                for v in range(TILES):
                    act.wait_ge(h_ps_done, c * TILES + v + 1)
                    after(act, h_lo_done, c * TILES + v - 1)
                    act.activation(h_full[:, v % 2, :], h_ps[v % 2][:, 0:T], exp).then_inc(h_exp, 1)
                    if not first:
                        if v == 3:
                            exps2(c - 1)
                        if v == 6:
                            attn2_t_round(c - 1)
                            t_round(c - 1, 1 - par, 0)
                        if v == 8:
                            out_exp(c - 1, 0)
                            t_round(c - 1, 1 - par, 1)
                        if v == 10:
                            out_exp(c - 1, 1)
                    if not last:
                        if v in (1, 3, 5, 7):
                            x_round(c + 1, v // 2)
                        if v == 9:
                            exps(c + 1)
                        if v == 12:
                            attn_t_round(c + 1, 0)
                        if v == 14:
                            attn_t_round(c + 1, 1)
                    act.wait_ge(h_elu, c * TILES + v + 1)
                    after(act, t_done, c * TILES + v - LAG)
                    act.activation(h_hi[:, v % RING, :], h_full[:, v % 2, :], copy).then_inc(h_hi_done, 1)

            for i, (_, hi, _) in enumerate(tiles):
                act.wait_ge(stage_in[i % 4], 16 * (i // 4 + 1))
                act.activation(hi, stage[i % 4], copy).then_inc(stage_hi, 1)
            for b in range(CB):
                x_round(0, b)
            exps(0)
            attn_t_round(0, 0)
            attn_t_round(0, 1)
            chunks(act, iteration)
            c, par = CHUNKS - 1, (CHUNKS - 1) % 2
            exps2(c)
            attn2_t_round(c)
            t_round(c, par, 0)
            out_exp(c, 0)
            t_round(c, par, 1)
            out_exp(c, 1)

        @block.vector
        def _(dve):
            tt, ts, stt = nc.vector.tensor_tensor, nc.vector.tensor_scalar, nc.vector.scalar_tensor_tensor

            def logits_out(c, p):
                dve.wait_ge(logits_ps, c * CP + p + 1)
                after(dve, diag_done, c)
                nc.vector.tensor_copy(logits[:, p, :], x_ps[0][:, 0:2 * NH]).then_inc(logits_sb, 1)

            def scores(c):
                dve.wait_ge(spread_ps, c + 1)
                dve.wait_ge(logits_sb, (c + 1) * CP)
                spread_view = x_ps[0][:, :].rearrange("p (a h n) -> p a h n", a=CP, h=NH)
                f1 = logits[:, :, 0:NH].unsqueeze(3).to_broadcast([P, CP, NH, N])
                sc, base = scores_g, c * 6
                tt(attn[:, :, :, 0, :], spread_view, f1, ALU.add).then_inc(front_step, 1)
                dve.wait_ge(front_step, base + 1)
                stt(sc, sc, ALPHA, sc, ALU.mult, ALU.max).then_inc(front_step, 1)
                dve.wait_ge(front_step, base + 2)
                tt(sc, sc, limit[:, :].unsqueeze(1).to_broadcast([P, CP * NH, N]), ALU.min)\
                    .then_inc(front_step, 1)
                dve.wait_ge(front_step, base + 3)
                nc.vector.tensor_reduce(row_max[:, :], sc, AX, ALU.max).then_inc(front_step, 1)
                dve.wait_ge(front_step, base + 4)
                tt(sc, sc, row_max[:, :].unsqueeze(2).to_broadcast([P, CP * NH, N]), ALU.subtract)\
                    .then_inc(scores_done, 1)

            def normalise(c):
                base = c * 6 + 4
                dve.wait_ge(exps_done, c + 1)
                nc.vector.tensor_reduce(row_sum[:, :], scores_g, AX, ALU.add).then_inc(front_step, 1)
                dve.wait_ge(front_step, base + 1)
                nc.vector.reciprocal(row_inv[:, :], row_sum[:, :]).then_inc(front_step, 1)
                dve.wait_ge(front_step, base + 2)
                inv = row_inv[:, :].unsqueeze(2).to_broadcast([P, CP * NH, N])
                tt(attn_copy, scores_g, inv, ALU.mult)
                tt(scores_g, scores_g, inv, ALU.mult).then_inc(attn_done, 1)

            def attn_t_rest(c, p):
                dve.wait_ge(attn_t_hi_done, c * CP + p + 1)
                hi, lo = (s[:, p, :, :].rearrange("p h n -> p (h n)") for s in (attn_t_hi, attn_t_lo))
                tt(lo, x_ps[0][:, :], hi.bitcast(F32), ALU.subtract).then_inc(attn_t_lo_done, 1)

            def g_rest(c, q):
                ft, p = q // CP, q % CP
                dve.wait_ge(g_hi_done, c * GQ + q + 1)
                hi, lo = (s[:, :, ft, p * P:(p + 1) * P].rearrange("p h (b n) -> p b h n", b=2)
                          for s in (g_hi, g_lo))
                tt(lo, x_ps[q % 2][:, :].rearrange("p (b h n) -> p b h n", b=2, h=NH), hi.bitcast(F32),
                   ALU.subtract).then_inc(g_lo_done, 1)

            def logits2_of(c, par):
                dve.wait_ge(t_done, (c + 1) * TILES)
                dve.wait_ge(a_row_in, 16 * (NH + 1))
                after(dve, mid_out, c * CP * 16)
                after(dve, diag2_done, c)
                base = c * (2 * CP - 1 + 6)
                for k in range(2 * CP):
                    p, j = k // 2, k % 2
                    done, by = (logits2_done, 1) if k == 2 * CP - 1 else (tail_step, 1)
                    if k:
                        dve.wait_ge(tail_step, base + k)
                    nc.vector.tensor_tensor_reduce(
                        out=o_buf[:, :], in0=t_ps[par][p][:, :], in1=a_row[:, j, :], scale=1.0, scalar=0.0,
                        op0=ALU.mult, op1=ALU.add, accum_out=logits2[:, j, p:p + 1]).then_inc(done, by)

            def scores2(c):
                base = c * (2 * CP - 1 + 6) + 2 * CP - 1
                sc, flat = attn2[:, :, :], attn2[:, :, :].rearrange("p a n -> p (a n)")
                dve.wait_ge(spread2_ps, c + 1)
                dve.wait_ge(logits2_done, c + 1)
                tt(sc, x_ps[1][:, 0:P].rearrange("p (a n) -> p a n", a=CP),
                   logits2[:, 0, :].unsqueeze(2).to_broadcast([P, CP, N]), ALU.add).then_inc(tail_step, 1)
                dve.wait_ge(tail_step, base + 1)
                stt(flat, flat, ALPHA, flat, ALU.mult, ALU.max).then_inc(tail_step, 1)
                dve.wait_ge(tail_step, base + 2)
                tt(sc, sc, limit[:, :].unsqueeze(1).to_broadcast([P, CP, N]), ALU.min).then_inc(tail_step, 1)
                dve.wait_ge(tail_step, base + 3)
                nc.vector.tensor_reduce(row_max2[:, :], sc, AX, ALU.max).then_inc(tail_step, 1)
                dve.wait_ge(tail_step, base + 4)
                tt(sc, sc, row_max2[:, :].unsqueeze(2).to_broadcast([P, CP, N]), ALU.subtract)\
                    .then_inc(scores2_done, 1)

            def normalise2(c):
                base = c * (2 * CP - 1 + 6) + 2 * CP - 1 + 4
                dve.wait_ge(exps2_done, c + 1)
                nc.vector.tensor_reduce(row_sum2[:, :], attn2[:, :, :], AX, ALU.add).then_inc(tail_step, 1)
                dve.wait_ge(tail_step, base + 1)
                nc.vector.reciprocal(row_inv2[:, :], row_sum2[:, :]).then_inc(tail_step, 1)
                dve.wait_ge(tail_step, base + 2)
                for half in range(2):
                    rows = slice(half * N, (half + 1) * N)
                    last = tt(attn2_bd[rows, :, half * N:(half + 1) * N], attn2[rows, :, :],
                              row_inv2[rows, :].unsqueeze(2).to_broadcast([N, CP, N]), ALU.mult)
                last.then_inc(attn2_done, 1)

            def attn2_t_rest(c):
                dve.wait_ge(attn2_t_hi_done, c + 1)
                hi, lo = (s[:, :, :].rearrange("p a n -> p (a n)") for s in (attn2_t_hi, attn2_t_lo))
                tt(lo, x_ps[1][:, 0:CP * P], hi.bitcast(F32), ALU.subtract).then_inc(attn2_t_lo_done, 1)

            def t_rest(c, par, p):
                dve.wait_ge(t_hi_done, c * CP + p + 1)
                tt(t_lo[:, :], t_ps[par][p][:, :], t_hi[:, :].bitcast(F32), ALU.subtract)\
                    .then_inc(t_lo_done, 1)

            def out_elu(c, p):
                dve.wait_ge(o_exp, c * CP + p + 1)
                ts(o_buf[:, :], o_buf[:, :], 1.0, -1.0, ALU.min, ALU.add).then_inc(o_min, 1)
                dve.wait_ge(o_min, c * CP + p + 1)
                tt(o_buf[:, :], x_ps[1][:, :], o_buf[:, :], ALU.max).then_inc(o_elu, 1)

            def iteration(c, par, first, last):
                for q in range(GQ):
                    g_rest(c, q)
                if not first:
                    logits2_of(c - 1, 1 - par)
                for v in range(TILES):
                    dve.wait_ge(h_exp, c * TILES + v + 1)
                    full = h_full[:, v % 2, :]
                    ts(full, full, 1.0, -1.0, ALU.min, ALU.add).then_inc(h_min, 1)
                    dve.wait_ge(h_min, c * TILES + v + 1)
                    tt(full, h_ps[v % 2][:, 0:T], full, ALU.max).then_inc(h_elu, 1)
                    if not first:
                        if v == 2:
                            scores2(c - 1)
                        if v == 4:
                            normalise2(c - 1)
                        if v == 6:
                            attn2_t_rest(c - 1)
                            t_rest(c - 1, 1 - par, 0)
                        if v == 8:
                            out_elu(c - 1, 0)
                            t_rest(c - 1, 1 - par, 1)
                        if v == 10:
                            out_elu(c - 1, 1)
                    if not last:
                        if v == 2:
                            logits_out(c + 1, 0)
                        if v == 4:
                            logits_out(c + 1, 1)
                        if v == 7:
                            scores(c + 1)
                        if v == 10:
                            normalise(c + 1)
                        if v == 12:
                            attn_t_rest(c + 1, 0)
                        if v == 14:
                            attn_t_rest(c + 1, 1)

            dve.wait_ge(adj_in, 32)
            ts(limit[:, :], adj_i[:, :], 0.0, OPEN, ALU.is_gt, ALU.mult).then_inc(limit_done, 1)
            dve.wait_ge(limit_done, 1)
            ts(limit[:, :], limit[:, :], MASKED, None, ALU.add).then_inc(limit_done, 1)
            dve.wait_ge(limit_done, 2)
            nc.vector.memset(attn2_bd[:, :, :], 0.0)
            for i, (_, hi, lo) in enumerate(tiles):
                dve.wait_ge(stage_in[i % 4], 16 * (i // 4 + 1))
                if i < HEAD_TILES:
                    h, ft = i // FT, i % FT
                    dve.wait_ge(a_row_in, 16 * (h + 1))
                    for j in range(2):
                        after(dve, u_done, 2 * i + j - 1)
                        nc.vector.tensor_tensor_reduce(
                            out=h_ps[j][:, :], in0=stage[i % 4], in1=a_row[:, j, :], scale=1.0, scalar=0.0,
                            op0=ALU.mult, op1=ALU.add, accum_out=u[:, ft, j * NH + h:j * NH + h + 1])\
                            .then_inc(u_done, 1)
                dve.wait_ge(stage_hi, i + 1)
                tt(lo, stage[i % 4], hi.bitcast(F32), ALU.subtract).then_inc(stage_lo, 1)
            logits_out(0, 0)
            logits_out(0, 1)
            scores(0)
            normalise(0)
            attn_t_rest(0, 0)
            attn_t_rest(0, 1)
            chunks(dve, iteration)
            c, par = CHUNKS - 1, (CHUNKS - 1) % 2
            logits2_of(c, par)
            scores2(c)
            normalise2(c)
            attn2_t_rest(c)
            t_rest(c, par, 0)
            out_elu(c, 0)
            t_rest(c, par, 1)
            out_elu(c, 1)

        @block.gpsimd
        def _(pool):
            tt = nc.gpsimd.tensor_tensor

            def x_rest(c, b):
                n = c * CB + b
                pool.wait_ge(x_hi_done, n + 1)
                rest = x_split[N:P, b, :]
                tt(rest, x_dup[N:P, :], rest.bitcast(F32), ALU.subtract).then_inc(x_lo_done, 1)
                pool.wait_ge(x_lo_done, n + 1)

            def diagonal(c):
                pool.wait_ge(logits_sb, (c + 1) * CP)
                pool.wait_ge(logits_ps, (c + 1) * CP)
                for p in range(CP):
                    last = tt(attn[:, p, :, 0, :], logits[:, p, NH:2 * NH].unsqueeze(2).to_broadcast([P, NH, N]),
                              node_ident[:, :].unsqueeze(1).to_broadcast([P, NH, N]), ALU.mult)
                last.then_inc(diag_done, 1)

            def diagonal2(c):
                pool.wait_ge(logits2_done, c + 1)
                after(pool, attn2_done, c)
                tt(attn2[:, :, :], logits2[:, 1, :].unsqueeze(2).to_broadcast([P, CP, N]),
                   node_ident[:, :].unsqueeze(1).to_broadcast([P, CP, N]), ALU.mult).then_inc(diag2_done, 1)

            def iteration(c, par, first, last):
                if not first:
                    diagonal2(c - 1)
                for v in range(TILES):
                    pool.wait_ge(h_hi_done, c * TILES + v + 1)
                    tt(h_lo[:, v % RING, :], h_full[:, v % 2, :], h_hi[:, v % RING, :].bitcast(F32),
                       ALU.subtract).then_inc(h_lo_done, 1)
                    if not last:
                        if v in (2, 4, 6, 8):
                            pool.wait_ge(h_lo_done, c * TILES + v + 1)
                            x_rest(c + 1, v // 2 - 1)
                        if v == 5:
                            diagonal(c + 1)

            nc.gpsimd.memset(same_batch[:, :], 0.0).then_inc(const_step, 1)
            nc.gpsimd.memset(ident[:, :], 0.0).then_inc(const_step, 1)
            pool.wait_ge(const_step, 2)
            nc.gpsimd.memset(same_batch[0:N, 0:N], 1.0).then_inc(const_step, 1)
            pool.wait_ge(const_step, 3)
            nc.gpsimd.memset(same_batch[N:P, N:P], 1.0).then_inc(const_step, 1)
            pool.wait_ge(const_step, 4)
            nc.gpsimd.affine_select(out=ident[:, :], in_=ident[:, :], compare_op=ALU.not_equal, fill=1.0,
                                    base=0, pattern=[[-1, P]], channel_multiplier=1)\
                .then_inc(const_step, 1)
            pool.wait_ge(const_step, 5)
            tt(node_ident[:, :], ident[:, 0:N], ident[:, N:P], ALU.add).then_inc(const_done, 1)
            pool.wait_ge(const_done, 1)
            for b in range(CB):
                x_rest(0, b)
            diagonal(0)
            chunks(pool, iteration)
            diagonal2(CHUNKS - 1)


def ffn_block(nc, x, w1, b1, w2, b2, gamma, beta, mid, out):
    import concourse.bass as bass
    from concourse import mybir

    F32, F32R = mybir.dt.float32, mybir.dt.float32r
    ALU, ACT = mybir.AluOpType, mybir.ActivationFunctionType

    P = 128
    F, D = w1.shape
    FT, DT = F // P, D // P
    CP = 2
    T = CP * P
    CHUNKS = x.shape[0] // T
    EPS = 1e-5
    x_v = x.rearrange("(a p) f -> p a f", p=P)
    mid_v = mid.rearrange("(a p) f -> p a f", p=P)

    with ExitStack() as ctx:
        def sb(name, shape, dt=F32):
            return ctx.enter_context(nc.sbuf_tensor(name, shape, dt))

        def sem(name):
            return ctx.enter_context(nc.semaphore(name))

        w1_f = sb("w1_f", [P, FT, D])
        w2_f = sb("w2_f", [P, DT, F])
        w1_hi, w1_lo = sb("w1_hi", [P, FT, D], F32R), sb("w1_lo", [P, FT, D], F32R)
        w2_hi, w2_lo = sb("w2_hi", [P, DT, F], F32R), sb("w2_lo", [P, DT, F], F32R)
        b1_col = sb("b1_col", [P, DT])
        b2_row, gamma_row, beta_row = sb("b2_row", [P, F]), sb("gamma_row", [P, F]), sb("beta_row", [P, F])
        ident = sb("ident2", [P, P])
        o_in = sb("o_in", [P, 2, CP, F])
        x_in = sb("x_in_b", [P, 2, CP, F])
        ob = sb("ob", [P, CP, F])
        xb = sb("xb", [P, CP, F])
        ot_hi, ot_lo = sb("ot_hi", [P, FT, T], F32R), sb("ot_lo", [P, FT, T], F32R)
        hid = sb("hid", [P, 2, T])
        hid_hi, hid_lo = sb("hid_hi", [P, DT, T], F32R), sb("hid_lo", [P, DT, T], F32R)
        y = sb("y", [P, CP, F])
        z = sb("z", [P, CP, F])
        res = sb("res", [P, CP, F])
        stats = sb("stats", [P, 2, 6])
        moments = sb("moments", [P, 2, 2])
        spread = sb("spread_b", [P, 2, 2])
        eps = sb("eps", [P, 1])

        def bank(name):
            return ctx.enter_context(nc.psum_tensor(name, [P, 512], F32))

        ot_ps = [bank(f"ot_ps{k}") for k in range(2)]
        hid_ps = [bank(f"hid_ps{k}") for k in range(2)]
        y_ps = [bank(f"y_ps{k}") for k in range(2)]

        w_in, row_in, o_load, x_load, store = (
            sem("w_in"), sem("row_in"), [sem(f"o_load{k}") for k in range(2)],
            [sem(f"x_load{k}") for k in range(2)], [sem(f"store{p}") for p in range(CP)])
        w_hi, w_lo, eye0, eye = sem("w_hi"), sem("w_lo"), sem("eye0"), sem("eye")
        ot_ps_done, ot_hi_done, ot_lo_done = sem("ot_ps_done"), sem("ot_hi_done"), sem("ot_lo_done")
        hid_ps_done, hid_done, hid_hi_done, hid_lo_done = (
            sem("hid_ps_done"), sem("hid_done"), sem("hid_hi_done"), sem("hid_lo_done"))
        y_ps_done, ob_done, xb_done = sem("y_ps_done"), sem("ob_done"), sem("xb_done")
        y_done, mean_done, std_done, z_done = sem("y_done"), sem("mean_done"), sem("std_done"), sem("z_done")
        mean2_done, std2_done, res_done, norm_step = (
            sem("mean2_done"), sem("std2_done"), sem("res_done"), sem("norm_step"))

        aggr_turn = sem("aggr_turn")

        block = ctx.enter_context(nc.Block())

        def after(eng, what, count):
            if not isinstance(count, int) or count > 0:
                eng.wait_ge(what, count)

        def chunks(eng, iteration):
            iteration(0, 0, last=False)
            iteration(1, 1, last=False)
            with eng.Fori(1, CHUNKS // 2 - 1, 1) as i:
                iteration(i * 2, 0, last=False)
                iteration(i * 2 + 1, 1, last=False)
            iteration(CHUNKS - 2, 0, last=False)
            iteration(CHUNKS - 1, 1, last=True)

        @block.sync
        def _(sp):
            sp.dma_start(w1_f[:, :, :], w1.rearrange("(a p) d -> p a d", p=P)).then_inc(w_in, 16)
            sp.dma_start(w2_f[:, :, :], w2.rearrange("(a p) f -> p a f", p=P)).then_inc(w_in, 16)
            sp.dma_start(b1_col[:, :], b1).then_inc(row_in, 16)
            for to, row in ((b2_row, b2), (gamma_row, gamma), (beta_row, beta)):
                sp.dma_start(to[:, :], row.partition_broadcast(P)).then_inc(row_in, 16)

            def load(c, par):
                after(sp, ot_ps_done, (c - 1) * CP)
                after(sp, ob_done, (c - 1) * CP)
                after(sp, xb_done, (c - 1) * CP)
                sp.dma_start(o_in[:, par, :, :], mid_v[:, bass.ds(c * CP, CP), :]).then_inc(o_load[par], 16)
                sp.dma_start(x_in[:, par, :, :], x_v[:, bass.ds(c * CP, CP), :]).then_inc(x_load[par], 16)

            def save(c):
                for p in range(CP):
                    sp.wait_ge(res_done, c * CP + p + 1)
                    sp.dma_start(out[bass.ts(c * CP + p, P), :], res[:, p, :]).then_inc(store[p], 16)

            def iteration(c, par, last):
                if not last:
                    load(c + 1, 1 - par)
                save(c)

            load(0, 0)
            chunks(sp, iteration)
            for p in range(CP):
                sp.wait_ge(store[p], 16 * CHUNKS)

        @block.tensor
        def _(pe):
            mm, transpose = nc.tensor.matmul, nc.tensor.transpose

            def transpose_o(c, par, turn):
                pe.wait_ge(o_load[par], turn * 16)
                for p in range(CP):
                    after(pe, ot_lo_done, (c - 1) * CP + p + 1)
                    for ft in range(FT):
                        last = transpose(ot_ps[p][:, ft * P:(ft + 1) * P], o_in[:, par, p, ft * P:(ft + 1) * P],
                                         ident[:, :])
                    last.then_inc(ot_ps_done, 1)

            def iteration(c, par, last, next_turn):
                for dt in range(DT):
                    if dt == 0:
                        pe.wait_ge(ot_lo_done, (c + 1) * CP)
                    after(pe, hid_done, c * DT + dt - 1)
                    to = hid_ps[dt % 2][:, 0:T]
                    for ft in range(FT):
                        a, b = (w[:, ft, dt * P:(dt + 1) * P] for w in (w1_hi, w1_lo))
                        mm(to, a, ot_hi[:, ft, :], start=ft == 0, stop=False)
                        mm(to, a, ot_lo[:, ft, :], start=False, stop=False)
                        end = mm(to, b, ot_hi[:, ft, :], start=False, stop=ft == FT - 1)
                    end.then_inc(hid_ps_done, 1)
                if not last:
                    transpose_o(c + 1, 1 - par, next_turn)
                for p in range(CP):
                    after(pe, y_done, (c - 1) * CP + p + 1)
                    for dt in range(DT):
                        if p == 0:
                            pe.wait_ge(hid_lo_done, c * DT + dt + 1)
                        a, b = (s[:, dt, p * P:(p + 1) * P] for s in (hid_hi, hid_lo))
                        to = y_ps[p][:, :]
                        mm(to, a, w2_hi[:, dt, :], start=dt == 0, stop=False)
                        mm(to, a, w2_lo[:, dt, :], start=False, stop=False)
                        end = mm(to, b, w2_hi[:, dt, :], start=False, stop=dt == DT - 1)
                    end.then_inc(y_ps_done, 1)

            pe.wait_ge(eye, 2)
            transpose_o(0, 0, 1)
            pe.wait_ge(w_lo, 2)
            iteration(0, 0, False, 1)
            iteration(1, 1, False, 2)
            with pe.Fori(1, CHUNKS // 2 - 1, 1) as i:
                iteration(i * 2, 0, False, i + 1)
                iteration(i * 2 + 1, 1, False, i + 2)
            iteration(CHUNKS - 2, 0, False, CHUNKS // 2)
            iteration(CHUNKS - 1, 1, True, None)

        @block.scalar
        def _(act):
            def ot_round(c):
                for p in range(CP):
                    act.wait_ge(ot_ps_done, c * CP + p + 1)
                    after(act, hid_ps_done, c * DT)
                    act.activation(ot_hi[:, :, p * P:(p + 1) * P],
                                   ot_ps[p][:, :].rearrange("p (f n) -> p f n", f=FT), ACT.Copy)\
                        .then_inc(ot_hi_done, 1)

            def iteration(c, par, last):
                for dt in range(DT):
                    act.wait_ge(hid_ps_done, c * DT + dt + 1)
                    after(act, hid_lo_done, c * DT + dt - 1)
                    act.activation(hid[:, dt % 2, :], hid_ps[dt % 2][:, 0:T], ACT.Relu, bias=b1_col[:, dt:dt + 1])\
                        .then_inc(hid_done, 1)
                    act.wait_ge(hid_done, c * DT + dt + 1)
                    if dt == 0:
                        after(act, y_ps_done, c * CP)
                    act.activation(hid_hi[:, dt, :], hid[:, dt % 2, :], ACT.Copy).then_inc(hid_hi_done, 1)
                if not last:
                    ot_round(c + 1)
                for p in range(CP):
                    n = c * CP + p
                    act.wait_ge(mean_done, n + 1)
                    act.activation(spread[:, 0, 0:1], moments[:, 0, 1:2], ACT.Sqrt, bias=eps[:, :])\
                        .then_inc(std_done, 1)
                    act.wait_ge(mean2_done, n + 1)
                    act.activation(spread[:, 1, 0:1], moments[:, 1, 1:2], ACT.Sqrt, bias=eps[:, :])\
                        .then_inc(std2_done, 1)

            act.wait_ge(w_in, 32)
            act.activation(w1_hi[:, :, :], w1_f[:, :, :], ACT.Copy).then_inc(w_hi, 1)
            act.activation(w2_hi[:, :, :], w2_f[:, :, :], ACT.Copy).then_inc(w_hi, 1)
            act.wait_ge(eye, 2)
            act.wait_ge(row_in, 64)
            ot_round(0)
            chunks(act, iteration)

        @block.vector
        def _(dve):
            tt, ts, stt = nc.vector.tensor_tensor, nc.vector.tensor_scalar, nc.vector.scalar_tensor_tensor

            def ot_rest(c):
                for p in range(CP):
                    dve.wait_ge(ot_hi_done, c * CP + p + 1)
                    hi, lo = (s[:, :, p * P:(p + 1) * P] for s in (ot_hi, ot_lo))
                    tt(lo, ot_ps[p][:, :].rearrange("p (f n) -> p f n", f=FT), hi.bitcast(F32), ALU.subtract)\
                        .then_inc(ot_lo_done, 1)

            def norms(c, p):
                n = c * CP + p
                base = n * 5
                dve.wait_ge(y_ps_done, n + 1)
                dve.wait_ge(ob_done, n + 1)
                tt(y[:, p, :], y_ps[p][:, :], ob[:, p, :], ALU.add).then_inc(y_done, 1)
                dve.wait_ge(y_done, n + 1)
                nc.vector.bn_stats(stats[:, 0, :], y[:, p, :]).then_inc(norm_step, 1)
                dve.wait_ge(norm_step, base + 1)
                dve.sem_inc(aggr_turn, 1)
                nc.vector.bn_aggr(moments[:, 0, :], stats[:, 0, :]).then_inc(mean_done, 1)
                dve.wait_ge(mean_done, n + 1)
                stt(z[:, p, :], y[:, p, :], moments[:, 0, 0:1], gamma_row[:, :], ALU.subtract, ALU.mult)\
                    .then_inc(norm_step, 1)
                dve.wait_ge(std_done, n + 1)
                nc.vector.reciprocal(spread[:, 0, 1:2], spread[:, 0, 0:1]).then_inc(norm_step, 1)
                dve.wait_ge(norm_step, base + 3)
                dve.wait_ge(xb_done, n + 1)
                stt(z[:, p, :], z[:, p, :], spread[:, 0, 1:2], xb[:, p, :], ALU.mult, ALU.add)\
                    .then_inc(z_done, 1)
                dve.wait_ge(z_done, n + 1)
                nc.vector.bn_stats(stats[:, 1, :], z[:, p, :]).then_inc(norm_step, 1)
                dve.wait_ge(norm_step, base + 4)
                dve.sem_inc(aggr_turn, 1)
                nc.vector.bn_aggr(moments[:, 1, :], stats[:, 1, :]).then_inc(mean2_done, 1)
                dve.wait_ge(std2_done, n + 1)
                nc.vector.reciprocal(spread[:, 1, 1:2], spread[:, 1, 0:1]).then_inc(norm_step, 1)
                dve.wait_ge(norm_step, base + 5)
                after(dve, store[p], c * 16)
                ts(res[:, p, :], z[:, p, :], moments[:, 1, 0:1], spread[:, 1, 1:2], ALU.subtract, ALU.mult)\
                    .then_inc(res_done, 1)

            def iteration(c, par, last):
                if not last:
                    ot_rest(c + 1)
                for p in range(CP):
                    norms(c, p)

            nc.vector.memset(eps[:, :], EPS).then_inc(eye, 1)
            dve.wait_ge(w_hi, 1)
            tt(w1_lo[:, :, :], w1_f[:, :, :], w1_hi[:, :, :].bitcast(F32), ALU.subtract).then_inc(w_lo, 1)
            dve.wait_ge(w_hi, 2)
            tt(w2_lo[:, :, :], w2_f[:, :, :], w2_hi[:, :, :].bitcast(F32), ALU.subtract).then_inc(w_lo, 1)
            dve.wait_ge(row_in, 64)
            ot_rest(0)
            chunks(dve, iteration)

        @block.gpsimd
        def _(pool):
            tt = nc.gpsimd.tensor_tensor

            def sums(c, par, turn):
                for p in range(CP):
                    n = c * CP + p
                    pool.wait_ge(o_load[par], turn * 16)
                    after(pool, y_done, n - CP + 1)
                    tt(ob[:, p, :], o_in[:, par, p, :], b2_row[:, :], ALU.add).then_inc(ob_done, 1)
                    pool.wait_ge(x_load[par], turn * 16)
                    after(pool, z_done, n - CP + 1)
                    tt(xb[:, p, :], x_in[:, par, p, :], beta_row[:, :], ALU.add).then_inc(xb_done, 1)

            def iteration(c, par, turn):
                for dt in range(DT):
                    pool.wait_ge(hid_hi_done, c * DT + dt + 1)
                    after(pool, y_ps_done, c * CP)
                    tt(hid_lo[:, dt, :], hid[:, dt % 2, :], hid_hi[:, dt, :].bitcast(F32), ALU.subtract)\
                        .then_inc(hid_lo_done, 1)
                sums(c, par, turn)

            nc.gpsimd.memset(ident[:, :], 0.0).then_inc(eye0, 1)
            pool.wait_ge(eye0, 1)
            nc.gpsimd.affine_select(out=ident[:, :], in_=ident[:, :], compare_op=ALU.not_equal, fill=1.0,
                                    base=0, pattern=[[-1, P]], channel_multiplier=1).then_inc(eye, 1)
            pool.wait_ge(row_in, 64)
            iteration(0, 0, 1)
            iteration(1, 1, 1)
            with pool.Fori(1, CHUNKS // 2 - 1, 1) as i:
                iteration(i * 2, 0, i + 1)
                iteration(i * 2 + 1, 1, i + 1)
            iteration(CHUNKS - 2, 0, CHUNKS // 2)
            iteration(CHUNKS - 1, 1, CHUNKS // 2)


_INS = ["x", "x_t", "adj", "w_heads", "a_heads", "w_out", "a_out", "w1", "b1", "w2", "b2", "gamma", "beta"]


def kernel(**inputs):
    import concourse.bacc as bacc
    from concourse import mybir
    from concourse.bass_utils import run_bass_kernel_spmd as run

    a = {k.removeprefix("L0_gnn_"): np.asarray(v) for k, v in inputs.items()}
    batches, nodes, features = a["x"].shape
    x = a["x"].reshape(batches * nodes, features)
    x_t = x.reshape(-1, 128, features // 128, 128).transpose(0, 3, 2, 1).reshape(-1, features)
    arrays = {
        "x": x, "x_t": x_t, "adj": a["adj"], "w_heads": a["W_heads"], "a_heads": a["a_heads"],
        "w_out": a["W_out"], "a_out": a["a_out"].reshape(1, -1), "w1": a["w1"],
        "b1": a["b1"].reshape(-1, 128).T, "w2": a["w2"], "b2": a["b2"].reshape(1, -1),
        "gamma": a["ln_gamma"].reshape(1, -1), "beta": a["ln_beta"].reshape(1, -1),
    }
    arrays = {f"in_{k}": np.ascontiguousarray(v) for k, v in arrays.items()}
    nc = bacc.Bacc("TRN2", target_bir_lowering=False, num_devices=1)
    args = [nc.dram_tensor(f"in_{k}", arrays[f"in_{k}"].shape, mybir.dt.from_np(arrays[f"in_{k}"].dtype),
                           kind="ExternalInput").ap() for k in _INS]
    mid = nc.dram_tensor("mid", x.shape, mybir.dt.float32, kind="Internal").ap()
    out = nc.dram_tensor("out", x.shape, mybir.dt.float32, kind="ExternalOutput").ap()
    build(nc, *args, mid, out)
    r = run(nc, [arrays], core_ids=[0])
    return r.results[0]["out"].reshape(batches, nodes, features)
```

```python
from contextlib import ExitStack

import numpy as np


def build(nc, x, x_t, adj, w_heads, a_heads, w_out, a_out, w1, b1, w2, b2, gamma, beta, mid, out):
    layers_block(nc, x, x_t, adj, w_heads, a_heads, w_out, a_out, mid)
    ffn_block(nc, x, w1, b1, w2, b2, gamma, beta, mid, out)


def layers_block(nc, x, x_t, adj, w_heads, a_heads, w_out, a_out, mid):
    import concourse.bass as bass
    from concourse import mybir

    F32, F32R = mybir.dt.float32, mybir.dt.float32r
    ALU, ACT = mybir.AluOpType, mybir.ActivationFunctionType
    AX = mybir.AxisListType.X

    P = 128
    N = adj.shape[0]
    NH, F, O = w_heads.shape
    FT = F // P
    OT = O // P
    CB = 4
    CP = CB // 2
    T = CB * N
    CHUNKS = x.shape[0] // T
    TILES = NH * OT
    GQ = FT * CP
    LAG = 3
    RING = LAG + 1
    ALPHA = 0.01
    MASKED, OPEN = -1.0e9, 3.0e38
    assert 2 * N == P and T == 256 and F == 512 and O == 512 and CHUNKS % 2 == 0 and CHUNKS > 4

    with ExitStack() as ctx:
        def sb(name, shape, dt=F32):
            return ctx.enter_context(nc.sbuf_tensor(name, shape, dt))

        def sem(name):
            return ctx.enter_context(nc.semaphore(name))

        wh_hi = sb("wh_hi", [P, NH, FT, O], F32R)
        wh_lo = sb("wh_lo", [P, NH, FT, O], F32R)
        wo_hi = sb("wo_hi", [P, TILES, O], F32R)
        wo_lo = sb("wo_lo", [P, TILES, O], F32R)
        u = sb("u", [P, FT, 2 * NH])
        a_row = sb("a_row", [P, 2, O])
        x_dup = sb("x_dup", [P, F])
        x_split = sb("x_split", [P, CB, F], F32R)
        attn = sb("attn", [P, CP, NH, 2, N])
        attn_t_hi = sb("attn_t_hi", [P, CP, NH, P], F32R)
        attn_t_lo = sb("attn_t_lo", [P, CP, NH, P], F32R)
        g_hi = sb("g_hi", [P, NH, FT, T], F32R)
        g_lo = sb("g_lo", [P, NH, FT, T], F32R)
        h_full = sb("h_full", [P, 2, T])
        h_hi = sb("h_hi", [P, RING, T], F32R)
        h_lo = sb("h_lo", [P, RING, T], F32R)
        logits = sb("logits", [P, CP, 2 * NH])
        logits2 = sb("logits2", [P, 2, CP])
        attn2 = sb("attn2", [P, CP, N])
        attn2_bd = sb("attn2_bd", [P, CP, P])
        attn2_t_hi = sb("attn2_t_hi", [P, CP, P], F32R)
        attn2_t_lo = sb("attn2_t_lo", [P, CP, P], F32R)
        t_hi = sb("t_hi", [P, O], F32R)
        t_lo = sb("t_lo", [P, O], F32R)
        o_buf = sb("o_buf", [P, O])
        row_max = sb("row_max", [P, CP * NH])
        row_sum = sb("row_sum", [P, CP * NH])
        row_inv = sb("row_inv", [P, CP * NH])
        row_max2 = sb("row_max2", [P, CP])
        row_sum2 = sb("row_sum2", [P, CP])
        row_inv2 = sb("row_inv2", [P, CP])
        ident = sb("ident", [P, P])
        same_batch = sb("same_batch", [P, P])
        node_ident = sb("node_ident", [P, N])
        adj_i = sb("adj_i", [P, N], mybir.dt.int32)
        limit = sb("limit", [P, N])

        def bank(name):
            return ctx.enter_context(nc.psum_tensor(name, [P, 512], F32))

        t_ps = [[bank(f"t_ps{k}{p}") for p in range(CP)] for k in range(2)]
        h_ps = [bank(f"h_ps{k}") for k in range(2)]
        x_ps = [bank(f"x_ps{k}") for k in range(2)]
        g_banks = h_ps + x_ps

        adj_in, a_row_in, stage_in = sem("adj_in"), sem("a_row_in"), [sem(f"stage_in{k}") for k in range(4)]
        wo_in = [sem(f"wo_in{k}") for k in range(3)]
        x_in, x_t_in, mid_out = sem("x_in"), sem("x_t_in"), sem("mid_out")
        const_step, const_done, limit_done = sem("const_step"), sem("const_done"), sem("limit_done")
        wh_hi_done, wh_lo_done, u_done = sem("wh_hi_done"), sem("wh_lo_done"), sem("u_done")
        wo_hi_done, wo_lo_done = sem("wo_hi_done"), sem("wo_lo_done")
        x_hi_done, x_lo_done = sem("x_hi_done"), sem("x_lo_done")
        logits_ps, logits_sb = sem("logits_ps"), sem("logits_sb")
        diag_done, spread_ps, scores_done, exps_done = (
            sem("diag_done"), sem("spread_ps"), sem("scores_done"), sem("exps_done"))
        attn_done, attn_t_ps, attn_t_hi_done, attn_t_lo_done = (
            sem("attn_done"), sem("attn_t_ps"), sem("attn_t_hi_done"), sem("attn_t_lo_done"))
        front_step = sem("front_step")
        g_ps, g_hi_done, g_lo_done = sem("g_ps"), sem("g_hi_done"), sem("g_lo_done")
        h_ps_done, h_exp, h_min, h_elu, h_hi_done, h_lo_done, t_done = (
            sem("h_ps_done"), sem("h_exp"), sem("h_min"), sem("h_elu"), sem("h_hi_done"), sem("h_lo_done"),
            sem("t_done"))
        logits2_done, diag2_done, spread2_ps, scores2_done, exps2_done, attn2_done = (
            sem("logits2_done"), sem("diag2_done"), sem("spread2_ps"), sem("scores2_done"), sem("exps2_done"),
            sem("attn2_done"))
        attn2_t_ps, attn2_t_hi_done, attn2_t_lo_done = (
            sem("attn2_t_ps"), sem("attn2_t_hi_done"), sem("attn2_t_lo_done"))
        t_hi_done, t_lo_done, o_ps, o_exp, o_min, o_elu = (
            sem("t_hi_done"), sem("t_lo_done"), sem("o_ps"), sem("o_exp"), sem("o_min"), sem("o_elu"))
        tail_step = sem("tail_step")

        block = ctx.enter_context(nc.Block())

        attn_flat = attn[:, :, :, :, :].rearrange("p a h d n -> p (a h d n)")
        attn_g = attn[:, :, :, :, :].rearrange("p a h d n -> p (a h) d n")
        scores_g, attn_copy = attn_g[:, :, 0, :], attn_g[:, :, 1, :]
        stage = [attn_flat[:, 0:F], attn_flat[:, F:2 * F], h_full[:, :, :].rearrange("p a t -> p (a t)"),
                 x_dup[:, :]]
        wo_stage = [o_buf[:, :], a_row[:, 0, :], a_row[:, 1, :]]
        tiles = [(w_heads[h, ft * P:(ft + 1) * P, :], wh_hi[:, h, ft, :], wh_lo[:, h, ft, :])
                 for h in range(NH) for ft in range(FT)]
        HEAD_TILES = NH * FT

        def after(eng, what, count):
            if not isinstance(count, int) or count > 0:
                eng.wait_ge(what, count)

        def chunks(eng, iteration):
            iteration(0, 0, first=True, last=False)
            iteration(1, 1, first=False, last=False)
            with eng.Fori(1, CHUNKS // 2 - 1, 1) as i:
                iteration(i * 2, 0, first=False, last=False)
                iteration(i * 2 + 1, 1, first=False, last=False)
            iteration(CHUNKS - 2, 0, first=False, last=False)
            iteration(CHUNKS - 1, 1, first=False, last=True)

        @block.sync
        def _(sp):
            for half in range(2):
                sp.dma_start(adj_i[half * N:(half + 1) * N, :], adj).then_inc(adj_in, 16)
            for i, (source, _, _) in enumerate(tiles):
                if i % FT == 0:
                    h = i // FT
                    after(sp, u_done, 2 * FT * h)
                    sp.dma_start(a_row[:, :, :].rearrange("p a o -> p (a o)"),
                                 a_heads[h:h + 1, :].partition_broadcast(P)).then_inc(a_row_in, 16)
                if i >= 4:
                    sp.wait_ge(wh_lo_done, i - 3)
                    sp.wait_ge(u_done, 2 * (i - 3))
                sp.dma_start(stage[i % 4], source).then_inc(stage_in[i % 4], 16)
            sp.wait_ge(wh_lo_done, HEAD_TILES)
            sp.wait_ge(u_done, 2 * HEAD_TILES)

            def load_x(c, b):
                after(sp, x_lo_done, c * CB + b)
                for half in range(2):
                    sp.dma_start(x_dup[half * N:(half + 1) * N, :],
                                 x[bass.ts(c * CB + b, N), :]).then_inc(x_in, 16)

            def load_x_t(c, p):
                if p == 0:
                    after(sp, attn_t_ps, c * CP)
                sp.dma_start(attn_flat[:, p * F:(p + 1) * F], x_t[bass.ts(c * CP + p, P), :])\
                    .then_inc(x_t_in, 16)

            def front(c):
                for p in range(CP):
                    load_x_t(c, p)
                for b in range(CB):
                    load_x(c, b)

            def tail(c):
                for p in range(CP):
                    sp.wait_ge(o_elu, c * CP + p + 1)
                    sp.dma_start(mid[bass.ts(c * CP + p, P), :], o_buf[:, :]).then_inc(mid_out, 16)

            def iteration(c, par, first, last):
                if not last:
                    front(c + 1)
                if first:
                    sp.wait_ge(wo_lo_done, TILES)
                    sp.dma_start(a_row[:, :, :].rearrange("p a o -> p (a o)"),
                                 a_out[0:1, :].partition_broadcast(P)).then_inc(a_row_in, 16)
                else:
                    tail(c - 1)

            front(0)
            chunks(sp, iteration)
            tail(CHUNKS - 1)
            sp.wait_ge(mid_out, 16 * CP * CHUNKS)

        @block.tensor
        def _(pe):
            mm, transpose = nc.tensor.matmul, nc.tensor.transpose

            def logits_of(c):
                pe.wait_ge(x_t_in, (c + 1) * CP * 16)
                after(pe, g_lo_done, c * GQ - 1)
                for p in range(CP):
                    for ft in range(FT):
                        last = mm(x_ps[0][:, p * 2 * NH:(p + 1) * 2 * NH],
                                  attn_flat[:, p * F + ft * P:p * F + (ft + 1) * P], u[:, ft, :],
                                  start=ft == 0, stop=ft == FT - 1)
                last.then_inc(logits_ps, 1)

            def spread(c):
                pe.wait_ge(diag_done, c + 1)
                mm(x_ps[0][:, :], same_batch[:, :], scores_g, start=True, stop=True).then_inc(spread_ps, 1)

            def transpose_attn(c, p):
                if p == 0:
                    pe.wait_ge(attn_done, c + 1)
                else:
                    pe.wait_ge(attn_t_lo_done, c * CP + p)
                for h in range(NH):
                    twice = attn[:, p, h, :, :].rearrange("p d n -> p (d n)")
                    last = transpose(x_ps[0][:, h * P:(h + 1) * P], twice, ident[:, :])
                last.then_inc(attn_t_ps, 1)

            def gather(c, q):
                ft, p = q // CP, q % CP
                if q == 0:
                    pe.wait_ge(attn_t_lo_done, c * CP + CP)
                    pe.wait_ge(x_lo_done, (c + 1) * CB)
                if q < 2:
                    after(pe, h_elu, c * TILES - 1 + q)
                elif q == 3:
                    after(pe, o_elu, (c - 1) * CP)
                elif q > 3:
                    pe.wait_ge(g_lo_done, c * GQ + q - 3)
                for b in range(2):
                    to = g_banks[q % 4][:, b * T:(b + 1) * T]
                    xb = x_split[:, 2 * p + b, ft * P:(ft + 1) * P]
                    mm(to, xb, attn_t_hi[:, p, :, b * N:(b + 1) * N], start=True, stop=False)
                    last = mm(to, xb, attn_t_lo[:, p, :, b * N:(b + 1) * N], start=False, stop=True)
                last.then_inc(g_ps, 1)

            def head(c, v):
                h, ot = v // OT, v % OT
                after(pe, h_elu, c * TILES + v - 1)
                to = h_ps[v % 2][:, 0:T]
                if v == 1:
                    pe.wait_ge(g_lo_done, (c + 1) * GQ)
                for ft in range(FT):
                    if v == 0:
                        pe.wait_ge(g_lo_done, c * GQ + max((ft + 1) * CP, 5))
                    w_hi = wh_hi[:, h, ft, ot * P:(ot + 1) * P]
                    w_lo = wh_lo[:, h, ft, ot * P:(ot + 1) * P]
                    mm(to, w_hi, g_hi[:, h, ft, :], start=ft == 0, stop=False)
                    mm(to, w_hi, g_lo[:, h, ft, :], start=False, stop=False)
                    last = mm(to, w_lo, g_hi[:, h, ft, :], start=False, stop=ft == FT - 1)
                last.then_inc(h_ps_done, 1)

            def add_out(c, par, v, first=False):
                pe.wait_ge(h_lo_done, c * TILES + v + 1)
                if first:
                    pe.wait_ge(wo_lo_done, v + 1)
                if v == 0:
                    after(pe, t_lo_done, (c - 1) * CP)
                for p in range(CP):
                    hh, hl = (s[:, v % RING, p * P:(p + 1) * P] for s in (h_hi, h_lo))
                    to = t_ps[par][p][:, :]
                    mm(to, hh, wo_hi[:, v, :], start=v == 0, stop=False)
                    mm(to, hh, wo_lo[:, v, :], start=False, stop=False)
                    last = mm(to, hl, wo_hi[:, v, :], start=False, stop=v == TILES - 1)
                last.then_inc(t_done, 1)

            def spread2(c, in_loop):
                pe.wait_ge(diag2_done, c + 1)
                if in_loop:
                    pe.wait_ge(g_lo_done, (c + 2) * GQ)
                else:
                    after(pe, o_elu, c * CP)
                mm(x_ps[1][:, 0:P], same_batch[:, :], attn2[:, :, :], start=True, stop=True)\
                    .then_inc(spread2_ps, 1)

            def transpose_attn2(c):
                pe.wait_ge(attn2_done, c + 1)
                for p in range(CP):
                    last = transpose(x_ps[1][:, p * P:(p + 1) * P], attn2_bd[:, p, :], ident[:, :])
                last.then_inc(attn2_t_ps, 1)

            def attend2(c, p):
                pe.wait_ge(t_lo_done, c * CP + p + 1)
                if p == 0:
                    pe.wait_ge(attn2_t_lo_done, c + 1)
                else:
                    pe.wait_ge(o_elu, c * CP + p)
                to = x_ps[1][:, :]
                mm(to, attn2_t_hi[:, p, :], t_hi[:, :], start=True, stop=False)
                mm(to, attn2_t_hi[:, p, :], t_lo[:, :], start=False, stop=False)
                mm(to, attn2_t_lo[:, p, :], t_hi[:, :], start=False, stop=True).then_inc(o_ps, 1)

            def iteration(c, par, first, last):
                second = isinstance(c, int) and c == 1
                for q in range(GQ):
                    if q in (0, 4) and not first:
                        add_out(c - 1, 1 - par, TILES - LAG + q // 4, second)
                    gather(c, q)
                if not first:
                    add_out(c - 1, 1 - par, TILES - 1, second)
                for v in range(TILES):
                    head(c, v)
                    if v >= LAG:
                        add_out(c, par, v - LAG, first)
                    if not first:
                        if v == 3:
                            spread2(c - 1, True)
                        if v == 9:
                            transpose_attn2(c - 1)
                        if v == 11:
                            attend2(c - 1, 0)
                        if v == 14:
                            attend2(c - 1, 1)
                    if not last:
                        if v == 1:
                            logits_of(c + 1)
                        if v == 6:
                            spread(c + 1)
                        if v == 11:
                            transpose_attn(c + 1, 0)
                        if v == 13:
                            transpose_attn(c + 1, 1)

            pe.wait_ge(u_done, 2 * HEAD_TILES)
            pe.wait_ge(const_done, 1)
            logits_of(0)
            spread(0)
            transpose_attn(0, 0)
            transpose_attn(0, 1)
            pe.wait_ge(wh_lo_done, HEAD_TILES)
            chunks(pe, iteration)
            for v in range(TILES - LAG, TILES):
                add_out(CHUNKS - 1, (CHUNKS - 1) % 2, v)
            spread2(CHUNKS - 1, False)
            transpose_attn2(CHUNKS - 1)
            attend2(CHUNKS - 1, 0)
            attend2(CHUNKS - 1, 1)

        @block.scalar
        def _(act):
            copy, exp = ACT.Copy, ACT.Exp

            def g_round(c, q):
                ft, p = q // CP, q % CP
                if q == 0:
                    after(act, h_ps_done, c * TILES)
                act.wait_ge(g_ps, c * GQ + q + 1)
                to = g_hi[:, :, ft, p * P:(p + 1) * P].rearrange("p h (b n) -> p b h n", b=2)
                act.activation(to, g_banks[q % 4][:, :].rearrange("p (b h n) -> p b h n", b=2, h=NH), copy)\
                    .then_inc(g_hi_done, 1)

            def x_round(c, b):
                act.wait_ge(x_in, (c * CB + b + 1) * 32)
                if b == 0:
                    after(act, g_ps, c * GQ)
                act.activation(x_split[:, b, :], x_dup[:, :], copy).then_inc(x_hi_done, 1)

            def exps(c):
                act.wait_ge(scores_done, c + 1)
                act.activation(scores_g, scores_g, exp).then_inc(exps_done, 1)

            def attn_t_round(c, p):
                act.wait_ge(attn_t_ps, c * CP + p + 1)
                after(act, g_ps, c * GQ)
                act.activation(attn_t_hi[:, p, :, :].rearrange("p h n -> p (h n)"), x_ps[0][:, :], copy)\
                    .then_inc(attn_t_hi_done, 1)

            def exps2(c):
                act.wait_ge(scores2_done, c + 1)
                act.activation(attn2[:, :, :], attn2[:, :, :], exp).then_inc(exps2_done, 1)

            def attn2_t_round(c):
                act.wait_ge(attn2_t_ps, c + 1)
                after(act, o_ps, c * CP)
                act.activation(attn2_t_hi[:, :, :].rearrange("p a n -> p (a n)"), x_ps[1][:, 0:CP * P], copy)\
                    .then_inc(attn2_t_hi_done, 1)

            def t_round(c, par, p):
                if p == 0:
                    act.wait_ge(t_done, (c + 1) * TILES)
                after(act, o_ps, c * CP + p)
                act.activation(t_hi[:, :], t_ps[par][p][:, :], copy).then_inc(t_hi_done, 1)

            def out_exp(c, p):
                act.wait_ge(o_ps, c * CP + p + 1)
                act.wait_ge(logits2_done, c + 1)
                after(act, mid_out, (c * CP + p) * 16)
                act.activation(o_buf[:, :], x_ps[1][:, :], exp).then_inc(o_exp, 1)

            def iteration(c, par, first, last):
                for q in range(GQ):
                    g_round(c, q)
                for v in range(TILES):
                    act.wait_ge(h_ps_done, c * TILES + v + 1)
                    after(act, h_lo_done, c * TILES + v - 1)
                    act.activation(h_full[:, v % 2, :], h_ps[v % 2][:, 0:T], exp).then_inc(h_exp, 1)
                    if first:
                        wo_round(v)
                        if v > 0 and v + 2 < TILES:
                            act.wait_ge(wo_lo_done, v)
                            load_wo(v + 2)
                    else:
                        if v == 6:
                            exps2(c - 1)
                        if v == 10:
                            attn2_t_round(c - 1)
                            t_round(c - 1, 1 - par, 0)
                        if v == 12:
                            out_exp(c - 1, 0)
                            t_round(c - 1, 1 - par, 1)
                        if v == 15:
                            out_exp(c - 1, 1)
                    if not last:
                        if v in (1, 4, 7, 10):
                            x_round(c + 1, v // 3)
                        if v == 8:
                            exps(c + 1)
                        if v == 12:
                            attn_t_round(c + 1, 0)
                        if v == 14:
                            attn_t_round(c + 1, 1)
                    act.wait_ge(h_elu, c * TILES + v + 1)
                    after(act, t_done, c * TILES + v - LAG)
                    act.activation(h_hi[:, v % RING, :], h_full[:, v % 2, :], copy).then_inc(h_hi_done, 1)

            def load_wo(k):
                act.dma_start(wo_stage[k % 3], w_out[k * P:(k + 1) * P, :]).then_inc(wo_in[k % 3], 16)

            def wo_round(k):
                act.wait_ge(wo_in[k % 3], 16 * (k // 3 + 1))
                act.activation(wo_hi[:, k, :], wo_stage[k % 3], copy).then_inc(wo_hi_done, 1)

            load_wo(0)
            for i, (_, hi, _) in enumerate(tiles):
                act.wait_ge(stage_in[i % 4], 16 * (i // 4 + 1))
                act.activation(hi, stage[i % 4], copy).then_inc(wh_hi_done, 1)
            act.wait_ge(u_done, 2 * HEAD_TILES)
            load_wo(1)
            load_wo(2)
            for b in range(CB):
                x_round(0, b)
            exps(0)
            attn_t_round(0, 0)
            attn_t_round(0, 1)
            chunks(act, iteration)
            c, par = CHUNKS - 1, (CHUNKS - 1) % 2
            exps2(c)
            attn2_t_round(c)
            t_round(c, par, 0)
            out_exp(c, 0)
            t_round(c, par, 1)
            out_exp(c, 1)

        @block.vector
        def _(dve):
            tt, ts, stt = nc.vector.tensor_tensor, nc.vector.tensor_scalar, nc.vector.scalar_tensor_tensor

            def logits_out(c):
                dve.wait_ge(logits_ps, c + 1)
                after(dve, diag_done, c)
                nc.vector.tensor_copy(logits[:, :, :].rearrange("p a k -> p (a k)"),
                                      x_ps[0][:, 0:CP * 2 * NH]).then_inc(logits_sb, 1)

            def scores(c):
                dve.wait_ge(spread_ps, c + 1)
                dve.wait_ge(logits_sb, c + 1)
                spread_view = x_ps[0][:, :].rearrange("p (a h n) -> p a h n", a=CP, h=NH)
                f1 = logits[:, :, 0:NH].unsqueeze(3).to_broadcast([P, CP, NH, N])
                sc, base = scores_g, c * 6
                tt(attn[:, :, :, 0, :], spread_view, f1, ALU.add).then_inc(front_step, 1)
                dve.wait_ge(front_step, base + 1)
                stt(sc, sc, ALPHA, sc, ALU.mult, ALU.max).then_inc(front_step, 1)
                dve.wait_ge(front_step, base + 2)
                tt(sc, sc, limit[:, :].unsqueeze(1).to_broadcast([P, CP * NH, N]), ALU.min)\
                    .then_inc(front_step, 1)
                dve.wait_ge(front_step, base + 3)
                nc.vector.tensor_reduce(row_max[:, :], sc, AX, ALU.max).then_inc(front_step, 1)
                dve.wait_ge(front_step, base + 4)
                tt(sc, sc, row_max[:, :].unsqueeze(2).to_broadcast([P, CP * NH, N]), ALU.subtract)\
                    .then_inc(scores_done, 1)

            def normalise(c):
                base = c * 6 + 4
                dve.wait_ge(exps_done, c + 1)
                nc.vector.tensor_reduce(row_sum[:, :], scores_g, AX, ALU.add).then_inc(front_step, 1)
                dve.wait_ge(front_step, base + 1)
                nc.vector.reciprocal(row_inv[:, :], row_sum[:, :]).then_inc(front_step, 1)
                dve.wait_ge(front_step, base + 2)
                inv = row_inv[:, :].unsqueeze(2).to_broadcast([P, CP * NH, N])
                tt(attn_copy, scores_g, inv, ALU.mult)
                tt(scores_g, scores_g, inv, ALU.mult).then_inc(attn_done, 1)

            def attn_t_rest(c, p):
                dve.wait_ge(attn_t_hi_done, c * CP + p + 1)
                hi, lo = (s[:, p, :, :].rearrange("p h n -> p (h n)") for s in (attn_t_hi, attn_t_lo))
                tt(lo, x_ps[0][:, :], hi.bitcast(F32), ALU.subtract).then_inc(attn_t_lo_done, 1)

            def g_rest(c, q):
                ft, p = q // CP, q % CP
                dve.wait_ge(g_hi_done, c * GQ + q + 1)
                hi, lo = (s[:, :, ft, p * P:(p + 1) * P].rearrange("p h (b n) -> p b h n", b=2)
                          for s in (g_hi, g_lo))
                tt(lo, g_banks[q % 4][:, :].rearrange("p (b h n) -> p b h n", b=2, h=NH), hi.bitcast(F32),
                   ALU.subtract).then_inc(g_lo_done, 1)

            def logits2_of(c, par, p):
                if p == 0:
                    dve.wait_ge(t_done, (c + 1) * TILES)
                    dve.wait_ge(a_row_in, 16 * (NH + 1))
                    after(dve, mid_out, c * CP * 16)
                    after(dve, diag2_done, c)
                base = c * (2 * CP - 1 + 6)
                for k in (2 * p, 2 * p + 1):
                    j = k % 2
                    done, by = (logits2_done, 1) if k == 2 * CP - 1 else (tail_step, 1)
                    if k:
                        dve.wait_ge(tail_step, base + k)
                    nc.vector.tensor_tensor_reduce(
                        out=o_buf[:, :], in0=t_ps[par][p][:, :], in1=a_row[:, j, :], scale=1.0, scalar=0.0,
                        op0=ALU.mult, op1=ALU.add, accum_out=logits2[:, j, p:p + 1]).then_inc(done, by)

            def scores2(c):
                base = c * (2 * CP - 1 + 6) + 2 * CP - 1
                sc, flat = attn2[:, :, :], attn2[:, :, :].rearrange("p a n -> p (a n)")
                dve.wait_ge(spread2_ps, c + 1)
                dve.wait_ge(logits2_done, c + 1)
                tt(sc, x_ps[1][:, 0:P].rearrange("p (a n) -> p a n", a=CP),
                   logits2[:, 0, :].unsqueeze(2).to_broadcast([P, CP, N]), ALU.add).then_inc(tail_step, 1)
                dve.wait_ge(tail_step, base + 1)
                stt(flat, flat, ALPHA, flat, ALU.mult, ALU.max).then_inc(tail_step, 1)
                dve.wait_ge(tail_step, base + 2)
                tt(sc, sc, limit[:, :].unsqueeze(1).to_broadcast([P, CP, N]), ALU.min).then_inc(tail_step, 1)
                dve.wait_ge(tail_step, base + 3)
                nc.vector.tensor_reduce(row_max2[:, :], sc, AX, ALU.max).then_inc(tail_step, 1)
                dve.wait_ge(tail_step, base + 4)
                tt(sc, sc, row_max2[:, :].unsqueeze(2).to_broadcast([P, CP, N]), ALU.subtract)\
                    .then_inc(scores2_done, 1)

            def normalise2(c):
                base = c * (2 * CP - 1 + 6) + 2 * CP - 1 + 4
                dve.wait_ge(exps2_done, c + 1)
                nc.vector.tensor_reduce(row_sum2[:, :], attn2[:, :, :], AX, ALU.add).then_inc(tail_step, 1)
                dve.wait_ge(tail_step, base + 1)
                nc.vector.reciprocal(row_inv2[:, :], row_sum2[:, :]).then_inc(tail_step, 1)
                dve.wait_ge(tail_step, base + 2)
                for half in range(2):
                    rows = slice(half * N, (half + 1) * N)
                    last = tt(attn2_bd[rows, :, half * N:(half + 1) * N], attn2[rows, :, :],
                              row_inv2[rows, :].unsqueeze(2).to_broadcast([N, CP, N]), ALU.mult)
                last.then_inc(attn2_done, 1)

            def attn2_t_rest(c):
                dve.wait_ge(attn2_t_hi_done, c + 1)
                hi, lo = (s[:, :, :].rearrange("p a n -> p (a n)") for s in (attn2_t_hi, attn2_t_lo))
                tt(lo, x_ps[1][:, 0:CP * P], hi.bitcast(F32), ALU.subtract).then_inc(attn2_t_lo_done, 1)

            def t_rest(c, par, p):
                dve.wait_ge(t_hi_done, c * CP + p + 1)
                tt(t_lo[:, :], t_ps[par][p][:, :], t_hi[:, :].bitcast(F32), ALU.subtract)\
                    .then_inc(t_lo_done, 1)

            def out_elu(c, p):
                dve.wait_ge(o_exp, c * CP + p + 1)
                ts(o_buf[:, :], o_buf[:, :], 1.0, -1.0, ALU.min, ALU.add).then_inc(o_min, 1)
                dve.wait_ge(o_min, c * CP + p + 1)
                tt(o_buf[:, :], x_ps[1][:, :], o_buf[:, :], ALU.max).then_inc(o_elu, 1)

            def iteration(c, par, first, last):
                for q in range(GQ):
                    g_rest(c, q)
                for v in range(TILES):
                    dve.wait_ge(h_exp, c * TILES + v + 1)
                    full = h_full[:, v % 2, :]
                    ts(full, full, 1.0, -1.0, ALU.min, ALU.add).then_inc(h_min, 1)
                    dve.wait_ge(h_min, c * TILES + v + 1)
                    tt(full, h_ps[v % 2][:, 0:T], full, ALU.max).then_inc(h_elu, 1)
                    if first:
                        dve.wait_ge(wo_hi_done, v + 1)
                        tt(wo_lo[:, v, :], wo_stage[v % 3], wo_hi[:, v, :].bitcast(F32), ALU.subtract)\
                            .then_inc(wo_lo_done, 1)
                    else:
                        if v < CP:
                            logits2_of(c - 1, 1 - par, v)
                        if v == 5:
                            scores2(c - 1)
                        if v == 7:
                            normalise2(c - 1)
                        if v == 10:
                            attn2_t_rest(c - 1)
                            t_rest(c - 1, 1 - par, 0)
                        if v == 12:
                            out_elu(c - 1, 0)
                            t_rest(c - 1, 1 - par, 1)
                        if v == 15:
                            out_elu(c - 1, 1)
                    if not last:
                        if v == 2:
                            logits_out(c + 1)
                        if v == 7:
                            scores(c + 1)
                        if v == 9:
                            normalise(c + 1)
                        if v == 12:
                            attn_t_rest(c + 1, 0)
                        if v == 14:
                            attn_t_rest(c + 1, 1)

            dve.wait_ge(adj_in, 32)
            ts(limit[:, :], adj_i[:, :], 0.0, OPEN, ALU.is_gt, ALU.mult).then_inc(limit_done, 1)
            dve.wait_ge(limit_done, 1)
            ts(limit[:, :], limit[:, :], MASKED, None, ALU.add).then_inc(limit_done, 1)
            dve.wait_ge(limit_done, 2)
            nc.vector.memset(attn2_bd[:, :, :], 0.0)
            for i in range(HEAD_TILES):
                h, ft = i // FT, i % FT
                dve.wait_ge(stage_in[i % 4], 16 * (i // 4 + 1))
                dve.wait_ge(a_row_in, 16 * (h + 1))
                for j in range(2):
                    after(dve, u_done, 2 * i + j - 1)
                    nc.vector.tensor_tensor_reduce(
                        out=h_ps[j][:, :], in0=stage[i % 4], in1=a_row[:, j, :], scale=1.0, scalar=0.0,
                        op0=ALU.mult, op1=ALU.add, accum_out=u[:, ft, j * NH + h:j * NH + h + 1])\
                        .then_inc(u_done, 1)
            logits_out(0)
            scores(0)
            normalise(0)
            attn_t_rest(0, 0)
            attn_t_rest(0, 1)
            chunks(dve, iteration)
            c, par = CHUNKS - 1, (CHUNKS - 1) % 2
            for p in range(CP):
                logits2_of(c, par, p)
            scores2(c)
            normalise2(c)
            attn2_t_rest(c)
            t_rest(c, par, 0)
            out_elu(c, 0)
            t_rest(c, par, 1)
            out_elu(c, 1)

        @block.gpsimd
        def _(pool):
            tt = nc.gpsimd.tensor_tensor

            def x_rest(c, b):
                n = c * CB + b
                pool.wait_ge(x_hi_done, n + 1)
                rest = x_split[N:P, b, :]
                tt(rest, x_dup[N:P, :], rest.bitcast(F32), ALU.subtract).then_inc(x_lo_done, 1)
                pool.wait_ge(x_lo_done, n + 1)

            def diagonal(c):
                pool.wait_ge(logits_sb, c + 1)
                pool.wait_ge(logits_ps, c + 1)
                tt(attn[:, :, :, 0, :], logits[:, :, NH:2 * NH].unsqueeze(3).to_broadcast([P, CP, NH, N]),
                   node_ident[:, :].unsqueeze(1).unsqueeze(1).to_broadcast([P, CP, NH, N]), ALU.mult)\
                    .then_inc(diag_done, 1)

            def diagonal2(c):
                pool.wait_ge(logits2_done, c + 1)
                after(pool, attn2_done, c)
                tt(attn2[:, :, :], logits2[:, 1, :].unsqueeze(2).to_broadcast([P, CP, N]),
                   node_ident[:, :].unsqueeze(1).to_broadcast([P, CP, N]), ALU.mult).then_inc(diag2_done, 1)

            def iteration(c, par, first, last):
                for v in range(TILES):
                    pool.wait_ge(h_hi_done, c * TILES + v + 1)
                    tt(h_lo[:, v % RING, :], h_full[:, v % 2, :], h_hi[:, v % RING, :].bitcast(F32),
                       ALU.subtract).then_inc(h_lo_done, 1)
                    if v == 1 and not first:
                        diagonal2(c - 1)
                    if not last:
                        if v in (2, 5, 8, 11):
                            pool.wait_ge(h_lo_done, c * TILES + v + 1)
                            x_rest(c + 1, v // 3)
                        if v == 3:
                            diagonal(c + 1)

            nc.gpsimd.memset(same_batch[:, :], 0.0).then_inc(const_step, 1)
            nc.gpsimd.memset(ident[:, :], 0.0).then_inc(const_step, 1)
            pool.wait_ge(const_step, 2)
            nc.gpsimd.memset(same_batch[0:N, 0:N], 1.0).then_inc(const_step, 1)
            pool.wait_ge(const_step, 3)
            nc.gpsimd.memset(same_batch[N:P, N:P], 1.0).then_inc(const_step, 1)
            pool.wait_ge(const_step, 4)
            nc.gpsimd.affine_select(out=ident[:, :], in_=ident[:, :], compare_op=ALU.not_equal, fill=1.0,
                                    base=0, pattern=[[-1, P]], channel_multiplier=1)\
                .then_inc(const_step, 1)
            pool.wait_ge(const_step, 5)
            tt(node_ident[:, :], ident[:, 0:N], ident[:, N:P], ALU.add).then_inc(const_done, 1)
            pool.wait_ge(const_done, 1)
            for i, (_, hi, lo) in enumerate(tiles):
                pool.wait_ge(wh_hi_done, i + 1)
                tt(lo, stage[i % 4], hi.bitcast(F32), ALU.subtract).then_inc(wh_lo_done, 1)
            pool.wait_ge(wh_lo_done, HEAD_TILES)
            for b in range(CB):
                x_rest(0, b)
            diagonal(0)
            chunks(pool, iteration)
            diagonal2(CHUNKS - 1)


def ffn_block(nc, x, w1, b1, w2, b2, gamma, beta, mid, out):
    import concourse.bass as bass
    from concourse import mybir

    F32, F32R = mybir.dt.float32, mybir.dt.float32r
    ALU, ACT = mybir.AluOpType, mybir.ActivationFunctionType

    P = 128
    F, D = w1.shape
    FT, DT = F // P, D // P
    CP = 2
    T = CP * P
    CHUNKS = x.shape[0] // T
    EPS = 1e-5
    x_v = x.rearrange("(a p) f -> p a f", p=P)
    mid_v = mid.rearrange("(a p) f -> p a f", p=P)

    with ExitStack() as ctx:
        def sb(name, shape, dt=F32):
            return ctx.enter_context(nc.sbuf_tensor(name, shape, dt))

        def sem(name):
            return ctx.enter_context(nc.semaphore(name))

        w1_f = sb("w1_f", [P, FT, D])
        w2_f = sb("w2_f", [P, DT, F])
        w1_hi, w1_lo = sb("w1_hi", [P, FT, D], F32R), sb("w1_lo", [P, FT, D], F32R)
        w2_hi, w2_lo = sb("w2_hi", [P, DT, F], F32R), sb("w2_lo", [P, DT, F], F32R)
        b1_col = sb("b1_col", [P, DT])
        b2_row, gamma_row, beta_row = sb("b2_row", [P, F]), sb("gamma_row", [P, F]), sb("beta_row", [P, F])
        ident = sb("ident2", [P, P])
        o_in = sb("o_in", [P, 2, CP, F])
        x_in = sb("x_in_b", [P, 2, CP, F])
        ob = sb("ob", [P, CP, F])
        xb = sb("xb", [P, CP, F])
        ot_hi, ot_lo = sb("ot_hi", [P, FT, T], F32R), sb("ot_lo", [P, FT, T], F32R)
        hid = sb("hid", [P, 2, T])
        hid_hi, hid_lo = sb("hid_hi", [P, DT, T], F32R), sb("hid_lo", [P, DT, T], F32R)
        y = sb("y", [P, CP, F])
        z = sb("z", [P, CP, F])
        res = sb("res", [P, CP, F])
        stats = sb("stats", [P, 2, CP, 6])
        moments = sb("moments", [P, 2, CP, 2])
        std = sb("std", [P, 2, CP])
        inv_std = sb("inv_std", [P, 2, CP])
        eps = sb("eps", [P, 1])

        def bank(name):
            return ctx.enter_context(nc.psum_tensor(name, [P, 512], F32))

        ot_ps = [bank(f"ot_ps{k}") for k in range(2)]
        hid_ps = [bank(f"hid_ps{k}") for k in range(2)]
        y_ps = [bank(f"y_ps{k}") for k in range(2)]

        w_in, row_in, o_load, x_load, store = (
            sem("w_in"), sem("row_in"), [sem(f"o_load{k}") for k in range(2)],
            [sem(f"x_load{k}") for k in range(2)], [sem(f"store{p}") for p in range(CP)])
        w_hi, w_lo, eye0, eye = sem("w_hi"), sem("w_lo"), sem("eye0"), sem("eye")
        ot_ps_done, ot_hi_done, ot_lo_done = sem("ot_ps_done"), sem("ot_hi_done"), sem("ot_lo_done")
        hid_ps_done, hid_done, hid_hi_done, hid_lo_done = (
            sem("hid_ps_done"), sem("hid_done"), sem("hid_hi_done"), sem("hid_lo_done"))
        y_ps_done, ob_done, xb_done = sem("y_ps_done"), sem("ob_done"), sem("xb_done")
        y_done, mean_done, std_done, z_done = sem("y_done"), sem("mean_done"), sem("std_done"), sem("z_done")
        mean2_done, std2_done, res_done = sem("mean2_done"), sem("std2_done"), sem("res_done")

        stats_done, inv_done = [sem(f"stats_done{k}") for k in range(2)], [sem(f"inv_done{k}") for k in range(2)]
        scaled, aggr_turn = sem("scaled"), sem("aggr_turn")

        block = ctx.enter_context(nc.Block())

        def after(eng, what, count):
            if not isinstance(count, int) or count > 0:
                eng.wait_ge(what, count)

        def first_of(c):
            return isinstance(c, int) and c == 0

        def chunks(eng, iteration):
            iteration(0, 0, last=False)
            iteration(1, 1, last=False)
            with eng.Fori(1, CHUNKS // 2 - 1, 1) as i:
                iteration(i * 2, 0, last=False)
                iteration(i * 2 + 1, 1, last=False)
            iteration(CHUNKS - 2, 0, last=False)
            iteration(CHUNKS - 1, 1, last=True)

        @block.sync
        def _(sp):
            sp.dma_start(w1_f[:, :, :], w1.rearrange("(a p) d -> p a d", p=P)).then_inc(w_in, 16)
            sp.dma_start(w2_f[:, :, :], w2.rearrange("(a p) f -> p a f", p=P)).then_inc(w_in, 16)
            sp.dma_start(b1_col[:, :], b1).then_inc(row_in, 16)
            for to, row in ((b2_row, b2), (gamma_row, gamma), (beta_row, beta)):
                sp.dma_start(to[:, :], row.partition_broadcast(P)).then_inc(row_in, 16)

            def load(c, par):
                after(sp, ot_ps_done, (c - 1) * CP)
                after(sp, ob_done, (c - 1) * CP)
                after(sp, xb_done, (c - 1) * CP)
                sp.dma_start(o_in[:, par, :, :], mid_v[:, bass.ds(c * CP, CP), :]).then_inc(o_load[par], 16)
                sp.dma_start(x_in[:, par, :, :], x_v[:, bass.ds(c * CP, CP), :]).then_inc(x_load[par], 16)

            def save(c):
                for p in range(CP):
                    sp.wait_ge(res_done, c * CP + p + 1)
                    sp.dma_start(out[bass.ts(c * CP + p, P), :], res[:, p, :]).then_inc(store[p], 16)

            def iteration(c, par, last):
                if not last:
                    load(c + 1, 1 - par)
                if not first_of(c):
                    save(c - 1)

            load(0, 0)
            chunks(sp, iteration)
            save(CHUNKS - 1)
            for p in range(CP):
                sp.wait_ge(store[p], 16 * CHUNKS)

        @block.tensor
        def _(pe):
            mm, transpose = nc.tensor.matmul, nc.tensor.transpose

            def transpose_o(c, par, turn):
                pe.wait_ge(o_load[par], turn * 16)
                for p in range(CP):
                    after(pe, ot_lo_done, (c - 1) * CP + p + 1)
                    for ft in range(FT):
                        last = transpose(ot_ps[p][:, ft * P:(ft + 1) * P], o_in[:, par, p, ft * P:(ft + 1) * P],
                                         ident[:, :])
                    last.then_inc(ot_ps_done, 1)

            def iteration(c, par, last, next_turn):
                for dt in range(DT):
                    if dt == 0:
                        pe.wait_ge(ot_lo_done, (c + 1) * CP)
                    after(pe, hid_done, c * DT + dt - 1)
                    to = hid_ps[dt % 2][:, 0:T]
                    for ft in range(FT):
                        a, b = (w[:, ft, dt * P:(dt + 1) * P] for w in (w1_hi, w1_lo))
                        mm(to, a, ot_hi[:, ft, :], start=ft == 0, stop=False)
                        mm(to, a, ot_lo[:, ft, :], start=False, stop=False)
                        end = mm(to, b, ot_hi[:, ft, :], start=False, stop=ft == FT - 1)
                    end.then_inc(hid_ps_done, 1)
                if not last:
                    transpose_o(c + 1, 1 - par, next_turn)
                for p in range(CP):
                    after(pe, y_done, (c - 1) * CP + p + 1)
                    for dt in range(DT):
                        if p == 0:
                            pe.wait_ge(hid_lo_done, c * DT + dt + 1)
                        a, b = (s[:, dt, p * P:(p + 1) * P] for s in (hid_hi, hid_lo))
                        to = y_ps[p][:, :]
                        mm(to, a, w2_hi[:, dt, :], start=dt == 0, stop=False)
                        mm(to, a, w2_lo[:, dt, :], start=False, stop=False)
                        end = mm(to, b, w2_hi[:, dt, :], start=False, stop=dt == DT - 1)
                    end.then_inc(y_ps_done, 1)

            pe.wait_ge(eye, 2)
            transpose_o(0, 0, 1)
            pe.wait_ge(w_lo, 2)
            iteration(0, 0, False, 1)
            iteration(1, 1, False, 2)
            with pe.Fori(1, CHUNKS // 2 - 1, 1) as i:
                iteration(i * 2, 0, False, i + 1)
                iteration(i * 2 + 1, 1, False, i + 2)
            iteration(CHUNKS - 2, 0, False, CHUNKS // 2)
            iteration(CHUNKS - 1, 1, True, None)

        @block.scalar
        def _(act):
            def ot_round(c):
                for p in range(CP):
                    act.wait_ge(ot_ps_done, c * CP + p + 1)
                    after(act, hid_ps_done, c * DT)
                    act.activation(ot_hi[:, :, p * P:(p + 1) * P],
                                   ot_ps[p][:, :].rearrange("p (f n) -> p f n", f=FT), ACT.Copy)\
                        .then_inc(ot_hi_done, 1)

            def deviation(c, k, ready, done):
                act.wait_ge(ready, (c + 1) * CP)
                act.activation(std[:, k, :], moments[:, k, :, 1], ACT.Sqrt, bias=eps[:, :]).then_inc(done, 1)

            def iteration(c, par, last):
                for dt in range(DT):
                    if dt == 2 and not first_of(c):
                        deviation(c - 1, 0, mean_done, std_done)
                    act.wait_ge(hid_ps_done, c * DT + dt + 1)
                    after(act, hid_lo_done, c * DT + dt - 1)
                    act.activation(hid[:, dt % 2, :], hid_ps[dt % 2][:, 0:T], ACT.Relu, bias=b1_col[:, dt:dt + 1])\
                        .then_inc(hid_done, 1)
                    act.wait_ge(hid_done, c * DT + dt + 1)
                    if dt == 0:
                        after(act, y_ps_done, c * CP)
                    act.activation(hid_hi[:, dt, :], hid[:, dt % 2, :], ACT.Copy).then_inc(hid_hi_done, 1)
                if not last:
                    ot_round(c + 1)
                if not first_of(c):
                    deviation(c - 1, 1, mean2_done, std2_done)
            act.wait_ge(w_in, 32)
            act.activation(w1_hi[:, :, :], w1_f[:, :, :], ACT.Copy).then_inc(w_hi, 1)
            act.activation(w2_hi[:, :, :], w2_f[:, :, :], ACT.Copy).then_inc(w_hi, 1)
            act.wait_ge(eye, 2)
            act.wait_ge(row_in, 64)
            ot_round(0)
            chunks(act, iteration)
            deviation(CHUNKS - 1, 0, mean_done, std_done)
            deviation(CHUNKS - 1, 1, mean2_done, std2_done)

        @block.vector
        def _(dve):
            tt, ts, stt = nc.vector.tensor_tensor, nc.vector.tensor_scalar, nc.vector.scalar_tensor_tensor

            def ot_rest(c):
                for p in range(CP):
                    dve.wait_ge(ot_hi_done, c * CP + p + 1)
                    hi, lo = (s[:, :, p * P:(p + 1) * P] for s in (ot_hi, ot_lo))
                    tt(lo, ot_ps[p][:, :].rearrange("p (f n) -> p f n", f=FT), hi.bitcast(F32), ALU.subtract)\
                        .then_inc(ot_lo_done, 1)

            def moments_of(c, k, source, step, ready):
                for p in range(CP):
                    dve.wait_ge(step, c * CP + p + 1)
                    nc.vector.bn_stats(stats[:, k, p, :], source[:, p, :]).then_inc(stats_done[k], 1)
                dve.wait_ge(stats_done[k], (c + 1) * CP)
                dve.sem_inc(aggr_turn, 1)
                for p in range(CP):
                    nc.vector.bn_aggr(moments[:, k, p, :], stats[:, k, p, :]).then_inc(ready, 1)

            def inverse(c, k, done):
                dve.wait_ge(done, c + 1)
                nc.vector.reciprocal(inv_std[:, k, :], std[:, k, :]).then_inc(inv_done[k], 1)
                dve.wait_ge(inv_done[k], c + 1)

            def norms(c, last):
                for p in range(CP):
                    dve.wait_ge(y_ps_done, c * CP + p + 1)
                    dve.wait_ge(ob_done, c * CP + p + 1)
                    tt(y[:, p, :], y_ps[p][:, :], ob[:, p, :], ALU.add).then_inc(y_done, 1)
                moments_of(c, 0, y, y_done, mean_done)
                for p in range(CP):
                    dve.wait_ge(mean_done, c * CP + p + 1)
                    stt(z[:, p, :], y[:, p, :], moments[:, 0, p, 0:1], gamma_row[:, :], ALU.subtract,
                        ALU.mult).then_inc(scaled, 1)
                inverse(c, 0, std_done)
                for p in range(CP):
                    dve.wait_ge(xb_done, c * CP + p + 1)
                    dve.wait_ge(scaled, c * CP + p + 1)
                    stt(z[:, p, :], z[:, p, :], inv_std[:, 0, p:p + 1], xb[:, p, :], ALU.mult, ALU.add)\
                        .then_inc(z_done, 1)
                moments_of(c, 1, z, z_done, mean2_done)
                if not last:
                    ot_rest(c + 2)
                inverse(c, 1, std2_done)
                for p in range(CP):
                    after(dve, store[p], c * 16)
                    dve.wait_ge(mean2_done, c * CP + p + 1)
                    ts(res[:, p, :], z[:, p, :], moments[:, 1, p, 0:1], inv_std[:, 1, p:p + 1],
                       ALU.subtract, ALU.mult).then_inc(res_done, 1)

            def iteration(c, par, last):
                if first_of(c):
                    ot_rest(1)
                else:
                    norms(c - 1, last)

            nc.vector.memset(eps[:, :], EPS).then_inc(eye, 1)
            dve.wait_ge(w_hi, 1)
            tt(w1_lo[:, :, :], w1_f[:, :, :], w1_hi[:, :, :].bitcast(F32), ALU.subtract).then_inc(w_lo, 1)
            dve.wait_ge(w_hi, 2)
            tt(w2_lo[:, :, :], w2_f[:, :, :], w2_hi[:, :, :].bitcast(F32), ALU.subtract).then_inc(w_lo, 1)
            dve.wait_ge(row_in, 64)
            ot_rest(0)
            chunks(dve, iteration)
            norms(CHUNKS - 1, True)

        @block.gpsimd
        def _(pool):
            tt = nc.gpsimd.tensor_tensor

            def sums(c, par, turn):
                for p in range(CP):
                    n = c * CP + p
                    pool.wait_ge(o_load[par], turn * 16)
                    after(pool, y_done, n - CP + 1)
                    tt(ob[:, p, :], o_in[:, par, p, :], b2_row[:, :], ALU.add).then_inc(ob_done, 1)
                    pool.wait_ge(x_load[par], turn * 16)
                    after(pool, z_done, n - CP + 1)
                    tt(xb[:, p, :], x_in[:, par, p, :], beta_row[:, :], ALU.add).then_inc(xb_done, 1)

            def iteration(c, par, turn):
                for dt in range(DT):
                    pool.wait_ge(hid_hi_done, c * DT + dt + 1)
                    after(pool, y_ps_done, c * CP)
                    tt(hid_lo[:, dt, :], hid[:, dt % 2, :], hid_hi[:, dt, :].bitcast(F32), ALU.subtract)\
                        .then_inc(hid_lo_done, 1)
                sums(c, par, turn)

            nc.gpsimd.memset(ident[:, :], 0.0).then_inc(eye0, 1)
            pool.wait_ge(eye0, 1)
            nc.gpsimd.affine_select(out=ident[:, :], in_=ident[:, :], compare_op=ALU.not_equal, fill=1.0,
                                    base=0, pattern=[[-1, P]], channel_multiplier=1).then_inc(eye, 1)
            pool.wait_ge(row_in, 64)
            iteration(0, 0, 1)
            iteration(1, 1, 1)
            with pool.Fori(1, CHUNKS // 2 - 1, 1) as i:
                iteration(i * 2, 0, i + 1)
                iteration(i * 2 + 1, 1, i + 1)
            iteration(CHUNKS - 2, 0, CHUNKS // 2)
            iteration(CHUNKS - 1, 1, CHUNKS // 2)


_INS = ["x", "x_t", "adj", "w_heads", "a_heads", "w_out", "a_out", "w1", "b1", "w2", "b2", "gamma", "beta"]


def kernel(**inputs):
    import concourse.bacc as bacc
    from concourse import mybir
    from concourse.bass_utils import run_bass_kernel_spmd as run

    a = {k.removeprefix("L0_gnn_"): np.asarray(v) for k, v in inputs.items()}
    batches, nodes, features = a["x"].shape
    x = a["x"].reshape(batches * nodes, features)
    x_t = x.reshape(-1, 128, features // 128, 128).transpose(0, 3, 2, 1).reshape(-1, features)
    arrays = {
        "x": x, "x_t": x_t, "adj": a["adj"], "w_heads": a["W_heads"], "a_heads": a["a_heads"],
        "w_out": a["W_out"], "a_out": a["a_out"].reshape(1, -1), "w1": a["w1"],
        "b1": a["b1"].reshape(-1, 128).T, "w2": a["w2"], "b2": a["b2"].reshape(1, -1),
        "gamma": a["ln_gamma"].reshape(1, -1), "beta": a["ln_beta"].reshape(1, -1),
    }
    arrays = {f"in_{k}": np.ascontiguousarray(v) for k, v in arrays.items()}
    nc = bacc.Bacc("TRN2", target_bir_lowering=False, num_devices=1)
    args = [nc.dram_tensor(f"in_{k}", arrays[f"in_{k}"].shape, mybir.dt.from_np(arrays[f"in_{k}"].dtype),
                           kind="ExternalInput").ap() for k in _INS]
    mid = nc.dram_tensor("mid", x.shape, mybir.dt.float32, kind="Internal").ap()
    out = nc.dram_tensor("out", x.shape, mybir.dt.float32, kind="ExternalOutput").ap()
    build(nc, *args, mid, out)
    r = run(nc, [arrays], core_ids=[0])
    return r.results[0]["out"].reshape(batches, nodes, features)
```

```python
from contextlib import ExitStack

import numpy as np


def build(nc, x, x_t, adj, w_heads, a_heads, w_out, a_out, w1, b1, w2, b2, gamma, beta, mid, out):
    import concourse.bass as bass
    from concourse import mybir

    F32, F32R = mybir.dt.float32, mybir.dt.float32r
    ALU, ACT = mybir.AluOpType, mybir.ActivationFunctionType
    AX = mybir.AxisListType.X

    P = 128
    N = adj.shape[0]
    NH, F, O = w_heads.shape
    FT = F // P
    OT = O // P
    CB = 4
    CP = CB // 2
    T = CB * N
    CHUNKS = x.shape[0] // T
    TILES = NH * OT
    GQ = FT * CP
    LAG = 3
    RING = LAG + 1
    ALPHA = 0.01
    MASKED, OPEN = -1.0e9, 3.0e38
    DT = w1.shape[1] // P
    EPS = 1e-5
    x_v = x.rearrange("(a p) f -> p a f", p=P)
    mid_v = mid.rearrange("(a p) f -> p a f", p=P)
    assert w1.shape == (O, DT * P) and w2.shape == (DT * P, F) and DT == FT and O == F
    assert CB == NH and 2 * N == P and T == 256 and F == 512 and O == 512 and CHUNKS % 2 == 0 and CHUNKS > 4

    with ExitStack() as ctx:
        def sb(name, shape, dt=F32):
            return ctx.enter_context(nc.sbuf_tensor(name, shape, dt))

        def sem(name):
            return ctx.enter_context(nc.semaphore(name))

        with nc.sbuf_tensor("wh_raw", [P, NH, FT, O], F32) as wh_raw, \
                nc.sbuf_tensor("wo_raw", [P, TILES, O], F32) as wo_raw:
            pass
        with ExitStack() as feed_forward:
            def sb_ff(name, shape, dt=F32):
                return feed_forward.enter_context(nc.sbuf_tensor(name, shape, dt))

            with nc.sbuf_tensor("w1_raw", [P, FT, DT * P], F32) as w1_raw, \
                    nc.sbuf_tensor("w2_raw", [P, DT, F], F32) as w2_raw:
                pass
            w1_lo, w2_lo = sb_ff("w1_lo", [P, FT, DT * P], F32R), sb_ff("w2_lo", [P, DT, F], F32R)
            hid_hi, hid_lo = sb_ff("hid_hi", [P, DT, T], F32R), sb_ff("hid_lo", [P, DT, T], F32R)
            x_again = sb_ff("x_again", [P, 2, CP, F])
            ob = sb_ff("ob", [P, CP, F])
            xb = sb_ff("xb", [P, CP, F])
            y, z, res = sb_ff("y", [P, CP, F]), sb_ff("z", [P, CP, F]), sb_ff("res", [P, CP, F])
            sb_ff("unused_wo", [P, 6, F])
            w1_hi, w2_hi = sb_ff("w1_hi", [P, FT, DT * P], F32R), sb_ff("w2_hi", [P, DT, F], F32R)
            b2_row, gamma_row, beta_row = (sb_ff("b2_row", [P, F]), sb_ff("gamma_row", [P, F]),
                                           sb_ff("beta_row", [P, F]))
            hid = sb_ff("hid", [P, 2, T])
            sb_ff("unused_wh", [P, 4, F])
            o_in = sb_ff("o_in", [P, 2, CP, F])
            ot_hi, ot_lo = sb_ff("ot_hi", [P, FT, T], F32R), sb_ff("ot_lo", [P, FT, T], F32R)
        wh_lo = sb("wh_lo", [P, NH, FT, O], F32R)
        wo_lo = sb("wo_lo", [P, TILES, O], F32R)
        wh_hi = sb("wh_hi", [P, NH, FT, O], F32R)
        x_split = sb("x_split", [P, CB, F], F32R)
        attn_t_hi = sb("attn_t_hi", [P, CP, NH, P], F32R)
        attn_t_lo = sb("attn_t_lo", [P, CP, NH, P], F32R)
        wo_hi = sb("wo_hi", [P, TILES, O], F32R)
        u = sb("u", [P, FT, 2 * NH])
        a_row = sb("a_row", [P, 2, O])
        x_dup = sb("x_dup", [P, F])
        with nc.sbuf_tensor("diag", [P, 2, CP, NH, N], F32R) as diag:
            pass
        attn = sb("attn", [P, CP, NH, 2, N])
        g_hi = sb("g_hi", [P, NH, FT, T], F32R)
        g_lo = sb("g_lo", [P, NH, FT, T], F32R)
        h_full = sb("h_full", [P, 2, T])
        h_hi = sb("h_hi", [P, RING, T], F32R)
        h_lo = sb("h_lo", [P, RING, T], F32R)
        logits = sb("logits", [P, CP, 2 * NH])
        logits2 = sb("logits2", [P, 2, CP])
        attn2 = sb("attn2", [P, CP, N])
        attn2_bd = sb("attn2_bd", [P, CP, P])
        attn2_t_hi = sb("attn2_t_hi", [P, CP, P], F32R)
        attn2_t_lo = sb("attn2_t_lo", [P, CP, P], F32R)
        t_hi = sb("t_hi", [P, O], F32R)
        t_lo = sb("t_lo", [P, O], F32R)
        o_buf = sb("o_buf", [P, O])
        row_max = sb("row_max", [P, CP * NH])
        row_sum = sb("row_sum", [P, CP * NH])
        row_inv = sb("row_inv", [P, CP * NH])
        row_max2 = sb("row_max2", [P, CP])
        row_sum2 = sb("row_sum2", [P, CP])
        row_inv2 = sb("row_inv2", [P, CP])
        b1_col = sb("b1_col", [P, DT])
        stats = sb("stats", [P, 2, CP, 6])
        moments = sb("moments", [P, 2, CP, 2])
        std = sb("std", [P, 2, CP])
        inv_std = sb("inv_std", [P, 2, CP])
        eps = sb("eps", [P, 1])
        ident = sb("ident", [P, P])
        same_batch = sb("same_batch", [P, P], F32R)
        node_ident = sb("node_ident", [P, N])
        with nc.sbuf_tensor("adj_i", [P, N], mybir.dt.int32) as adj_i:
            pass
        limit = sb("limit", [P, N])

        def bank(name):
            return ctx.enter_context(nc.psum_tensor(name, [P, 512], F32))

        t_ps = [[bank(f"t_ps{k}{p}") for p in range(CP)] for k in range(2)]
        h_ps = [bank(f"h_ps{k}") for k in range(2)]
        x_ps = [bank(f"x_ps{k}") for k in range(2)]
        g_banks = h_ps + x_ps
        ot_ps, hid_ps, y_ps = x_ps[0], h_ps, t_ps[CHUNKS % 2]

        adj_in, a_row_in = sem("adj_in"), sem("a_row_in")
        a_heads_in = [sem(f"a_heads_in{h}") for h in range(NH)]
        wh_in = [sem(f"wh_in{h}") for h in range(NH)]
        wo_in = [sem(f"wo_in{k}") for k in range(2)]
        x_in, x_t_in, mid_out = sem("x_in"), sem("x_t_in"), sem("mid_out")
        const_step, const_done, limit_done = sem("const_step"), sem("const_done"), sem("limit_done")
        wh_hi_done, wh_lo_done, u_done = sem("wh_hi_done"), sem("wh_lo_done"), sem("u_done")
        wo_hi_done, wo_lo_done = sem("wo_hi_done"), sem("wo_lo_done")
        x_hi_done, x_lo_done = sem("x_hi_done"), sem("x_lo_done")
        f2_step = sem("f2_step")
        logits_ps, logits_sb = sem("logits_ps"), sem("logits_sb")
        diag_done, spread_ps, scores_done, exps_done = (
            sem("diag_done"), sem("spread_ps"), sem("scores_done"), sem("exps_done"))
        attn_done, attn_t_ps, attn_t_hi_done, attn_t_lo_done = (
            sem("attn_done"), sem("attn_t_ps"), sem("attn_t_hi_done"), sem("attn_t_lo_done"))
        front_step = sem("front_step")
        g_ps, g_hi_done, g_lo_done = sem("g_ps"), sem("g_hi_done"), sem("g_lo_done")
        h_ps_done, h_exp, h_min, h_elu, h_hi_done, h_lo_done, t_done = (
            sem("h_ps_done"), sem("h_exp"), sem("h_min"), sem("h_elu"), sem("h_hi_done"), sem("h_lo_done"),
            sem("t_done"))
        logits2_done, diag2_done, spread2_ps, scores2_done, exps2_done, attn2_done = (
            sem("logits2_done"), sem("diag2_done"), sem("spread2_ps"), sem("scores2_done"), sem("exps2_done"),
            sem("attn2_done"))
        attn2_t_ps, attn2_t_hi_done, attn2_t_lo_done = (
            sem("attn2_t_ps"), sem("attn2_t_hi_done"), sem("attn2_t_lo_done"))
        t_hi_done, t_lo_done, o_ps, o_exp, o_min, o_elu = (
            sem("t_hi_done"), sem("t_lo_done"), sem("o_ps"), sem("o_exp"), sem("o_min"), sem("o_elu"))
        tail_step = sem("tail_step")

        w_in, row_in, o_load, x_load, store = (
            sem("w_in"), sem("row_in"), [sem(f"o_load{k}") for k in range(2)],
            [sem(f"x_load{k}") for k in range(2)], [sem(f"store{p}") for p in range(CP)])
        w_hi_done, w_lo_done = sem("w_hi_done"), sem("w_lo_done")
        ot_ps_done, ot_hi_done, ot_lo_done = sem("ot_ps_done"), sem("ot_hi_done"), sem("ot_lo_done")
        hid_ps_done, hid_done, hid_hi_done, hid_lo_done = (
            sem("hid_ps_done"), sem("hid_done"), sem("hid_hi_done"), sem("hid_lo_done"))
        y_ps_done, ob_done, xb_done = sem("y_ps_done"), sem("ob_done"), sem("xb_done")
        y_done, mean_done, std_done, z_done = sem("y_done"), sem("mean_done"), sem("std_done"), sem("z_done")
        mean2_done, std2_done, res_done, eps_done = (
            sem("mean2_done"), sem("std2_done"), sem("res_done"), sem("eps_done"))
        stats_done, inv_done = [sem(f"stats_done{k}") for k in range(2)], [sem(f"inv_done{k}") for k in range(2)]
        scaled, aggr_turn = sem("scaled"), sem("aggr_turn")

        block = ctx.enter_context(nc.Block())

        f2_hi, f2_lo = (s[:, :].rearrange("p (a h) -> p a h", a=CP) for s in (row_max, row_sum))
        attn_flat = attn[:, :, :, :, :].rearrange("p a h d n -> p (a h d n)")
        attn_g = attn[:, :, :, :, :].rearrange("p a h d n -> p (a h) d n")
        scores_g, attn_copy = attn_g[:, :, 0, :], attn_g[:, :, 1, :]
        HALF = TILES // 2
        a_all = wo_raw[:, HALF:HALF + 2 * NH, :]
        HEAD_TILES = NH * FT

        def after(eng, what, count):
            if not isinstance(count, int) or count > 0:
                eng.wait_ge(what, count)

        LAST = CHUNKS - 1
        LAYERS_TILES, LAYERS_PAIRS = CHUNKS * TILES, CHUNKS * CP

        def first_of(c):
            return isinstance(c, int) and c == 0

        def chunks(eng, iteration):
            iteration(0, 0, first=True, last=False)
            iteration(1, 1, first=False, last=False)
            with eng.Fori(1, CHUNKS // 2 - 1, 1) as i:
                iteration(i * 2, 0, first=False, last=False)
                iteration(i * 2 + 1, 1, first=False, last=False)
            iteration(CHUNKS - 2, 0, first=False, last=False)
            iteration(CHUNKS - 1, 1, first=False, last=True)

        @block.sync
        def _(sp):
            for half in range(2):
                sp.dma_start(adj_i[half * N:(half + 1) * N, :], adj).then_inc(adj_in, 16)
            def load_wo(k):
                part = slice(k * HALF, (k + 1) * HALF)
                sp.dma_start(wo_raw[:, part, :], w_out.rearrange("(v p) o -> p v o", p=P)[:, part, :])\
                    .then_inc(wo_in[k], 16)

            def load_x(c, b):
                after(sp, x_lo_done, c * CB + b)
                for half in range(2):
                    sp.dma_start(x_dup[half * N:(half + 1) * N, :],
                                 x[bass.ts(c * CB + b, N), :]).then_inc(x_in, 16)

            def load_x_t(c, p):
                if p == 0:
                    after(sp, attn_t_ps, c * CP)
                sp.dma_start(attn_flat[:, p * F:(p + 1) * F], x_t[bass.ts(c * CP + p, P), :])\
                    .then_inc(x_t_in, 16)

            def front(c):
                for p in range(CP):
                    load_x_t(c, p)
                for b in range(CB):
                    load_x(c, b)

            def tail(c):
                for p in range(CP):
                    sp.wait_ge(o_elu, c * CP + p + 1)
                    sp.dma_start(mid[bass.ts(c * CP + p, P), :], o_buf[:, :]).then_inc(mid_out, 16)

            def iteration(c, par, first, last):
                if not last:
                    front(c + 1)
                if last:
                    sp.wait_ge(g_ps, CHUNKS * GQ)
                    load_o(0, 0)
                    load_o(1, 1)
                    sp.wait_ge(h_ps_done, LAST * TILES + 2 * OT)
                    sp.dma_start(w1_raw[:, :, :], w1.rearrange("(a p) d -> p a d", p=P)).then_inc(w_in, 16)
                    sp.dma_start(w2_raw[:, :, :], w2.rearrange("(a p) f -> p a f", p=P)).then_inc(w_in, 16)
                if not first:
                    tail(c - 1)

            def load_o(c, par):
                after(sp, ot_ps_done, (c - 1) * CP)
                after(sp, ob_done, (c - 1) * CP)
                sp.wait_ge(mid_out, (c + 1) * CP * 16)
                sp.dma_start(o_in[:, par, :, :], mid_v[:, bass.ds(c * CP, CP), :]).then_inc(o_load[par], 16)

            def load_x_again(c, par):
                after(sp, xb_done, (c - 1) * CP)
                sp.dma_start(x_again[:, par, :, :], x_v[:, bass.ds(c * CP, CP), :]).then_inc(x_load[par], 16)

            def save(c):
                for p in range(CP):
                    sp.wait_ge(res_done, c * CP + p + 1)
                    sp.dma_start(out[bass.ts(c * CP + p, P), :], res[:, p, :]).then_inc(store[p], 16)

            def ff_iteration(c, par, first, last):
                if not last and not first:
                    load_o(c + 1, 1 - par)
                    load_x_again(c + 1, 1 - par)
                if isinstance(c, int) and c == 1:
                    tail(LAST)
                if not first:
                    save(c - 1)

            def load_head(h):
                sp.dma_start(a_all[:, 2 * h:2 * h + 2, :].rearrange("p k o -> p (k o)"),
                             a_heads[h:h + 1, :].partition_broadcast(P)).then_inc(a_heads_in[h], 16)
                sp.dma_start(wh_raw[:, h, :, :], w_heads[h].rearrange("(a p) o -> p a o", p=P))\
                    .then_inc(wh_in[h], 16)

            load_head(0)
            load_x(0, 0)
            load_head(1)
            load_head(2)
            for p in range(CP):
                load_x_t(0, p)
            load_head(3)
            for b in range(1, CB):
                load_x(0, b)
            load_wo(0)
            sp.dma_start(a_row[:, :, :].rearrange("p a o -> p (a o)"),
                         a_out[0:1, :].partition_broadcast(P)).then_inc(a_row_in, 16)
            sp.dma_start(b1_col[:, :], b1).then_inc(row_in, 16)
            sp.wait_ge(u_done, 2 * HEAD_TILES)
            load_wo(1)
            chunks(sp, iteration)
            sp.wait_ge(h_ps_done, LAYERS_TILES)
            for to, row in ((b2_row, b2), (gamma_row, gamma), (beta_row, beta)):
                sp.dma_start(to[:, :], row.partition_broadcast(P)).then_inc(row_in, 16)
            load_x_again(0, 0)
            load_x_again(1, 1)
            chunks(sp, ff_iteration)
            save(LAST)
            for p in range(CP):
                sp.wait_ge(store[p], 16 * CHUNKS)

        @block.tensor
        def _(pe):
            mm, transpose = nc.tensor.matmul, nc.tensor.transpose

            def logits_of(c):
                pe.wait_ge(x_t_in, (c + 1) * CP * 16)
                after(pe, g_lo_done, c * GQ - 1)
                for p in range(CP):
                    for ft in range(FT):
                        last = mm(x_ps[0][:, p * 2 * NH:(p + 1) * 2 * NH],
                                  attn_flat[:, p * F + ft * P:p * F + (ft + 1) * P], u[:, ft, :],
                                  start=ft == 0, stop=ft == FT - 1)
                last.then_inc(logits_ps, 1)

            def spread(c):
                pe.wait_ge(diag_done, (c + 1) * 2)
                for k in range(2):
                    last = mm(x_ps[0][:, :], same_batch[:, :], diag[:, k, :, :, :].rearrange("p a h n -> p (a h n)"),
                              start=k == 0, stop=k == 1)
                last.then_inc(spread_ps, 1)

            def transpose_attn(c, p):
                if p == 0:
                    pe.wait_ge(attn_done, c + 1)
                else:
                    pe.wait_ge(attn_t_lo_done, c * CP + p)
                for h in range(NH):
                    twice = attn[:, p, h, :, :].rearrange("p d n -> p (d n)")
                    last = transpose(x_ps[0][:, h * P:(h + 1) * P], twice, ident[:, :])
                last.then_inc(attn_t_ps, 1)

            def gather(c, q):
                ft, p = q // CP, q % CP
                if q == 0:
                    pe.wait_ge(attn_t_lo_done, c * CP + CP)
                    pe.wait_ge(x_lo_done, (c + 1) * CB)
                if q < 2:
                    after(pe, h_elu, c * TILES - 1 + q)
                elif q == 3:
                    after(pe, o_elu, (c - 1) * CP)
                elif q > 3:
                    pe.wait_ge(g_lo_done, c * GQ + q - 3)
                for b in range(2):
                    to = g_banks[q % 4][:, b * T:(b + 1) * T]
                    xb = x_split[:, 2 * p + b, ft * P:(ft + 1) * P]
                    mm(to, xb, attn_t_hi[:, p, :, b * N:(b + 1) * N], start=True, stop=False)
                    last = mm(to, xb, attn_t_lo[:, p, :, b * N:(b + 1) * N], start=False, stop=True)
                last.then_inc(g_ps, 1)

            def head(c, v):
                h, ot = v // OT, v % OT
                after(pe, h_elu, c * TILES + v - 1)
                to = h_ps[v % 2][:, 0:T]
                if v == 1:
                    pe.wait_ge(g_lo_done, (c + 1) * GQ)
                for ft in range(FT):
                    if v == 0:
                        pe.wait_ge(g_lo_done, c * GQ + max((ft + 1) * CP, 5))
                    w_hi = wh_hi[:, h, ft, ot * P:(ot + 1) * P]
                    w_lo = wh_lo[:, h, ft, ot * P:(ot + 1) * P]
                    mm(to, w_hi, g_hi[:, h, ft, :], start=ft == 0, stop=False)
                    mm(to, w_hi, g_lo[:, h, ft, :], start=False, stop=False)
                    last = mm(to, w_lo, g_hi[:, h, ft, :], start=False, stop=ft == FT - 1)
                last.then_inc(h_ps_done, 1)

            def add_out(c, par, v, first=False):
                pe.wait_ge(h_lo_done, c * TILES + v + 1)
                if first:
                    pe.wait_ge(wo_lo_done, v + 1)
                if v == 0:
                    after(pe, t_lo_done, (c - 1) * CP)
                for p in range(CP):
                    hh, hl = (s[:, v % RING, p * P:(p + 1) * P] for s in (h_hi, h_lo))
                    to = t_ps[par][p][:, :]
                    mm(to, hh, wo_hi[:, v, :], start=v == 0, stop=False)
                    mm(to, hh, wo_lo[:, v, :], start=False, stop=False)
                    last = mm(to, hl, wo_hi[:, v, :], start=False, stop=v == TILES - 1)
                last.then_inc(t_done, 1)

            def spread2(c, in_loop):
                pe.wait_ge(diag2_done, c + 1)
                if in_loop:
                    pe.wait_ge(g_lo_done, (c + 2) * GQ)
                else:
                    after(pe, o_elu, c * CP)
                mm(x_ps[1][:, 0:P], same_batch[:, :].bitcast(F32), attn2[:, :, :], start=True, stop=True)\
                    .then_inc(spread2_ps, 1)

            def transpose_attn2(c):
                pe.wait_ge(attn2_done, c + 1)
                for p in range(CP):
                    last = transpose(x_ps[1][:, p * P:(p + 1) * P], attn2_bd[:, p, :], ident[:, :])
                last.then_inc(attn2_t_ps, 1)

            def attend2(c, p):
                pe.wait_ge(t_lo_done, c * CP + p + 1)
                if p == 0:
                    pe.wait_ge(attn2_t_lo_done, c + 1)
                else:
                    pe.wait_ge(o_elu, c * CP + p)
                to = x_ps[1][:, :]
                mm(to, attn2_t_hi[:, p, :], t_hi[:, :], start=True, stop=False)
                mm(to, attn2_t_hi[:, p, :], t_lo[:, :], start=False, stop=False)
                mm(to, attn2_t_lo[:, p, :], t_hi[:, :], start=False, stop=True).then_inc(o_ps, 1)

            def iteration(c, par, first, last):
                second = isinstance(c, int) and c == 1
                for q in range(GQ):
                    if q in (0, 4) and not first:
                        add_out(c - 1, 1 - par, TILES - LAG + q // 4, second)
                    gather(c, q)
                if not first:
                    add_out(c - 1, 1 - par, TILES - 1, second)
                for v in range(TILES):
                    if first and v % OT == 0:
                        pe.wait_ge(wh_lo_done, FT * (v // OT + 1))
                    head(c, v)
                    if v >= LAG:
                        add_out(c, par, v - LAG, first)
                    if not first:
                        if v == 3:
                            spread2(c - 1, True)
                        if v == 9:
                            transpose_attn2(c - 1)
                        if v == 11:
                            attend2(c - 1, 0)
                        if v == 14:
                            attend2(c - 1, 1)
                    if not last:
                        if v == 1:
                            logits_of(c + 1)
                        if v == 6:
                            spread(c + 1)
                        if v == 11:
                            transpose_attn(c + 1, 0)
                        if v == 13:
                            transpose_attn(c + 1, 1)

            def transpose_o(c, par, turn, p):
                if p == 0:
                    pe.wait_ge(o_load[par], turn * 16)
                after(pe, ot_lo_done, c * CP + p)
                for ft in range(FT):
                    last = transpose(ot_ps[:, ft * P:(ft + 1) * P], o_in[:, par, p, ft * P:(ft + 1) * P],
                                     ident[:, :])
                last.then_inc(ot_ps_done, 1)

            def hidden(c, dt):
                if dt == 0:
                    pe.wait_ge(ot_lo_done, (c + 1) * CP)
                after(pe, hid_done, c * DT + dt - 1)
                to = hid_ps[dt % 2][:, 0:T]
                for ft in range(FT):
                    a, b = (w[:, ft, dt * P:(dt + 1) * P] for w in (w1_hi, w1_lo))
                    mm(to, a, ot_hi[:, ft, :], start=ft == 0, stop=False)
                    mm(to, a, ot_lo[:, ft, :], start=False, stop=False)
                    end = mm(to, b, ot_hi[:, ft, :], start=False, stop=ft == FT - 1)
                end.then_inc(hid_ps_done, 1)

            def result(c, p):
                after(pe, y_done, (c - 1) * CP + p + 1)
                if first_of(c):
                    pe.wait_ge(t_lo_done, LAST * CP)
                for dt in range(DT):
                    if p == 0:
                        pe.wait_ge(hid_lo_done, c * DT + dt + 1)
                    a, b = (s[:, dt, p * P:(p + 1) * P] for s in (hid_hi, hid_lo))
                    to = y_ps[p][:, :]
                    mm(to, a, w2_hi[:, dt, :], start=dt == 0, stop=False)
                    mm(to, a, w2_lo[:, dt, :], start=False, stop=False)
                    end = mm(to, b, w2_hi[:, dt, :], start=False, stop=dt == DT - 1)
                end.then_inc(y_ps_done, 1)

            def ff_iteration(c, par, last, next_turn):
                zeroth, second = first_of(c), isinstance(c, int) and c == 1
                if second:
                    attend2(LAST, 0)
                for dt in range(DT):
                    if zeroth and dt == 3:
                        spread2(LAST, False)
                    if second and dt == 2:
                        attend2(LAST, 1)
                    hidden(c, dt)
                for p in range(CP):
                    if zeroth and p == 1:
                        transpose_attn2(LAST)
                    if not last:
                        transpose_o(c + 1, 1 - par, next_turn, p)
                    result(c, p)

            pe.wait_ge(u_done, 2 * HEAD_TILES)
            pe.wait_ge(const_done, 1)
            logits_of(0)
            spread(0)
            transpose_attn(0, 0)
            transpose_attn(0, 1)
            chunks(pe, iteration)
            for v in range(TILES - LAG, TILES):
                add_out(LAST, LAST % 2, v)
                if v - (TILES - LAG) < CP:
                    transpose_o(0, 0, 1, v - (TILES - LAG))
            pe.wait_ge(w_lo_done, 2 * FT)
            pe.wait_ge(h_elu, LAYERS_TILES)
            ff_iteration(0, 0, False, 1)
            ff_iteration(1, 1, False, 2)
            with pe.Fori(1, CHUNKS // 2 - 1, 1) as i:
                ff_iteration(i * 2, 0, False, i + 1)
                ff_iteration(i * 2 + 1, 1, False, i + 2)
            ff_iteration(CHUNKS - 2, 0, False, CHUNKS // 2)
            ff_iteration(LAST, 1, True, None)

        @block.scalar
        def _(act):
            copy, exp = ACT.Copy, ACT.Exp

            def g_round(c, q):
                ft, p = q // CP, q % CP
                if q == 0:
                    after(act, h_ps_done, c * TILES)
                act.wait_ge(g_ps, c * GQ + q + 1)
                to = g_hi[:, :, ft, p * P:(p + 1) * P].rearrange("p h (b n) -> p b h n", b=2)
                act.activation(to, g_banks[q % 4][:, :].rearrange("p (b h n) -> p b h n", b=2, h=NH), copy)\
                    .then_inc(g_hi_done, 1)

            def x_round(c, b):
                act.wait_ge(x_in, (c * CB + b + 1) * 32)
                if b == 0:
                    after(act, g_ps, c * GQ)
                act.activation(x_split[:, b, :], x_dup[:, :], copy).then_inc(x_hi_done, 1)

            def exps(c):
                act.wait_ge(scores_done, c + 1)
                act.activation(scores_g, scores_g, exp).then_inc(exps_done, 1)

            def attn_t_round(c, p):
                act.wait_ge(attn_t_ps, c * CP + p + 1)
                after(act, g_ps, c * GQ)
                act.activation(attn_t_hi[:, p, :, :].rearrange("p h n -> p (h n)"), x_ps[0][:, :], copy)\
                    .then_inc(attn_t_hi_done, 1)

            def exps2(c):
                act.wait_ge(scores2_done, c + 1)
                act.activation(attn2[:, :, :], attn2[:, :, :], exp).then_inc(exps2_done, 1)

            def attn2_t_round(c):
                act.wait_ge(attn2_t_ps, c + 1)
                after(act, o_ps, c * CP)
                act.activation(attn2_t_hi[:, :, :].rearrange("p a n -> p (a n)"), x_ps[1][:, 0:CP * P], copy)\
                    .then_inc(attn2_t_hi_done, 1)

            def t_round(c, par, p):
                if p == 0:
                    act.wait_ge(t_done, (c + 1) * TILES)
                after(act, o_ps, c * CP + p)
                act.activation(t_hi[:, :], t_ps[par][p][:, :], copy).then_inc(t_hi_done, 1)

            def out_exp(c, p):
                act.wait_ge(o_ps, c * CP + p + 1)
                act.wait_ge(logits2_done, c + 1)
                after(act, mid_out, (c * CP + p) * 16)
                act.activation(o_buf[:, :], x_ps[1][:, :], exp).then_inc(o_exp, 1)

            def iteration(c, par, first, last):
                for q in range(GQ):
                    g_round(c, q)
                for v in range(TILES):
                    act.wait_ge(h_ps_done, c * TILES + v + 1)
                    after(act, h_lo_done, c * TILES + v - 1)
                    act.activation(h_full[:, v % 2, :], h_ps[v % 2][:, 0:T], exp).then_inc(h_exp, 1)
                    if first:
                        wo_round(v)
                    else:
                        if v == 6:
                            exps2(c - 1)
                        if v == 10:
                            attn2_t_round(c - 1)
                            t_round(c - 1, 1 - par, 0)
                        if v == 12:
                            out_exp(c - 1, 0)
                            t_round(c - 1, 1 - par, 1)
                        if v == 15:
                            out_exp(c - 1, 1)
                    if not last:
                        if v in (1, 4, 7, 10):
                            x_round(c + 1, v // 3)
                        if v == 8:
                            exps(c + 1)
                        if v == 12:
                            attn_t_round(c + 1, 0)
                        if v == 14:
                            attn_t_round(c + 1, 1)
                    elif v >= TILES - FT:
                        weights_round(v - (TILES - FT))
                    act.wait_ge(h_elu, c * TILES + v + 1)
                    after(act, t_done, c * TILES + v - LAG)
                    act.activation(h_hi[:, v % RING, :], h_full[:, v % 2, :], copy).then_inc(h_hi_done, 1)

            def weights_round(ft):
                act.wait_ge(w_in, 32)
                act.activation(w1_hi[:, ft, :], w1_raw[:, ft, :], copy).then_inc(w_hi_done, 1)
                act.activation(w2_hi[:, ft, :], w2_raw[:, ft, :], copy).then_inc(w_hi_done, 1)

            def ot_round(c, p):
                act.wait_ge(ot_ps_done, c * CP + p + 1)
                after(act, hid_ps_done, c * DT)
                act.activation(ot_hi[:, :, p * P:(p + 1) * P],
                               ot_ps[:, :].rearrange("p (f n) -> p f n", f=FT), copy).then_inc(ot_hi_done, 1)

            def deviation(c, k, ready, done):
                act.wait_ge(ready, (c + 1) * CP)
                act.activation(std[:, k, :], moments[:, k, :, 1], ACT.Sqrt, bias=eps[:, :]).then_inc(done, 1)

            def ff_iteration(c, par, first, last):
                second = isinstance(c, int) and c == 1
                if second:
                    out_exp(LAST, 0)
                    t_round(LAST, LAST % 2, 1)
                for dt in range(DT):
                    if dt == 2:
                        if second:
                            out_exp(LAST, 1)
                        if not first:
                            deviation(c - 1, 0, mean_done, std_done)
                    act.wait_ge(hid_ps_done, c * DT + dt + 1)
                    after(act, hid_lo_done, c * DT + dt - 1)
                    act.activation(hid[:, dt % 2, :], hid_ps[dt % 2][:, 0:T], ACT.Relu, bias=b1_col[:, dt:dt + 1])\
                        .then_inc(hid_done, 1)
                    act.wait_ge(hid_done, c * DT + dt + 1)
                    if dt == 0:
                        after(act, y_ps_done, c * CP)
                    act.activation(hid_hi[:, dt, :], hid[:, dt % 2, :], copy).then_inc(hid_hi_done, 1)
                if first:
                    exps2(LAST)
                if not last:
                    ot_round(c + 1, 0)
                if first:
                    attn2_t_round(LAST)
                    t_round(LAST, LAST % 2, 0)
                else:
                    deviation(c - 1, 1, mean2_done, std2_done)
                if not last:
                    ot_round(c + 1, 1)

            def wo_round(k):
                act.wait_ge(wo_in[k // HALF], 16)
                act.activation(wo_hi[:, k, :], wo_raw[:, k, :], copy).then_inc(wo_hi_done, 1)

            for h in range(NH):
                act.wait_ge(wh_in[h], 16)
                for ft in range(FT):
                    act.activation(wh_hi[:, h, ft, :], wh_raw[:, h, ft, :], copy).then_inc(wh_hi_done, 1)
                x_round(0, h)
            exps(0)
            attn_t_round(0, 0)
            attn_t_round(0, 1)
            chunks(act, iteration)
            for p in range(CP):
                ot_round(0, p)
            act.wait_ge(row_in, 64)
            act.wait_ge(eps_done, 1)
            chunks(act, ff_iteration)
            deviation(LAST, 0, mean_done, std_done)
            deviation(LAST, 1, mean2_done, std2_done)

        @block.vector
        def _(dve):
            tt, ts, stt = nc.vector.tensor_tensor, nc.vector.tensor_scalar, nc.vector.scalar_tensor_tensor

            def logits_out(c):
                dve.wait_ge(logits_ps, c + 1)
                after(dve, diag_done, c * 2)
                nc.vector.tensor_copy(logits[:, :, :].rearrange("p a k -> p (a k)"),
                                      x_ps[0][:, 0:CP * 2 * NH]).then_inc(f2_step, 1)
                f2 = logits[:, :, NH:2 * NH]
                dve.wait_ge(f2_step, c * 2 + 1)
                nc.vector.tensor_copy(f2_hi.bitcast(F32R), f2).then_inc(f2_step, 1)
                dve.wait_ge(f2_step, c * 2 + 2)
                tt(f2_lo, f2, f2_hi, ALU.subtract).then_inc(logits_sb, 1)

            def scores(c):
                dve.wait_ge(spread_ps, c + 1)
                dve.wait_ge(logits_sb, c + 1)
                spread_view = x_ps[0][:, :].rearrange("p (a h n) -> p a h n", a=CP, h=NH)
                f1 = logits[:, :, 0:NH].unsqueeze(3).to_broadcast([P, CP, NH, N])
                sc, base = scores_g, c * 6
                tt(attn[:, :, :, 0, :], spread_view, f1, ALU.add).then_inc(front_step, 1)
                dve.wait_ge(front_step, base + 1)
                stt(sc, sc, ALPHA, sc, ALU.mult, ALU.max).then_inc(front_step, 1)
                dve.wait_ge(front_step, base + 2)
                tt(sc, sc, limit[:, :].unsqueeze(1).to_broadcast([P, CP * NH, N]), ALU.min)\
                    .then_inc(front_step, 1)
                dve.wait_ge(front_step, base + 3)
                nc.vector.tensor_reduce(row_max[:, :], sc, AX, ALU.max).then_inc(front_step, 1)
                dve.wait_ge(front_step, base + 4)
                tt(sc, sc, row_max[:, :].unsqueeze(2).to_broadcast([P, CP * NH, N]), ALU.subtract)\
                    .then_inc(scores_done, 1)

            def normalise(c):
                base = c * 6 + 4
                dve.wait_ge(exps_done, c + 1)
                nc.vector.tensor_reduce(row_sum[:, :], scores_g, AX, ALU.add).then_inc(front_step, 1)
                dve.wait_ge(front_step, base + 1)
                nc.vector.reciprocal(row_inv[:, :], row_sum[:, :]).then_inc(front_step, 1)
                dve.wait_ge(front_step, base + 2)
                inv = row_inv[:, :].unsqueeze(2).to_broadcast([P, CP * NH, N])
                tt(attn_copy, scores_g, inv, ALU.mult)
                tt(scores_g, scores_g, inv, ALU.mult).then_inc(attn_done, 1)

            def attn_t_rest(c, p):
                dve.wait_ge(attn_t_hi_done, c * CP + p + 1)
                hi, lo = (s[:, p, :, :].rearrange("p h n -> p (h n)") for s in (attn_t_hi, attn_t_lo))
                tt(lo, x_ps[0][:, :], hi.bitcast(F32), ALU.subtract).then_inc(attn_t_lo_done, 1)

            def g_rest(c, q):
                ft, p = q // CP, q % CP
                dve.wait_ge(g_hi_done, c * GQ + q + 1)
                hi, lo = (s[:, :, ft, p * P:(p + 1) * P].rearrange("p h (b n) -> p b h n", b=2)
                          for s in (g_hi, g_lo))
                tt(lo, g_banks[q % 4][:, :].rearrange("p (b h n) -> p b h n", b=2, h=NH), hi.bitcast(F32),
                   ALU.subtract).then_inc(g_lo_done, 1)

            def logits2_of(c, par, p):
                if p == 0:
                    dve.wait_ge(t_done, (c + 1) * TILES)
                    dve.wait_ge(a_row_in, 16)
                    after(dve, mid_out, c * CP * 16)
                    after(dve, diag2_done, c)
                base = c * (2 * CP - 1 + 6)
                for k in (2 * p, 2 * p + 1):
                    j = k % 2
                    done, by = (logits2_done, 1) if k == 2 * CP - 1 else (tail_step, 1)
                    if k:
                        dve.wait_ge(tail_step, base + k)
                    nc.vector.tensor_tensor_reduce(
                        out=o_buf[:, :], in0=t_ps[par][p][:, :], in1=a_row[:, j, :], scale=1.0, scalar=0.0,
                        op0=ALU.mult, op1=ALU.add, accum_out=logits2[:, j, p:p + 1]).then_inc(done, by)

            def scores2(c):
                base = c * (2 * CP - 1 + 6) + 2 * CP - 1
                sc, flat = attn2[:, :, :], attn2[:, :, :].rearrange("p a n -> p (a n)")
                dve.wait_ge(spread2_ps, c + 1)
                dve.wait_ge(logits2_done, c + 1)
                tt(sc, x_ps[1][:, 0:P].rearrange("p (a n) -> p a n", a=CP),
                   logits2[:, 0, :].unsqueeze(2).to_broadcast([P, CP, N]), ALU.add).then_inc(tail_step, 1)
                dve.wait_ge(tail_step, base + 1)
                stt(flat, flat, ALPHA, flat, ALU.mult, ALU.max).then_inc(tail_step, 1)
                dve.wait_ge(tail_step, base + 2)
                tt(sc, sc, limit[:, :].unsqueeze(1).to_broadcast([P, CP, N]), ALU.min).then_inc(tail_step, 1)
                dve.wait_ge(tail_step, base + 3)
                nc.vector.tensor_reduce(row_max2[:, :], sc, AX, ALU.max).then_inc(tail_step, 1)
                dve.wait_ge(tail_step, base + 4)
                tt(sc, sc, row_max2[:, :].unsqueeze(2).to_broadcast([P, CP, N]), ALU.subtract)\
                    .then_inc(scores2_done, 1)

            def normalise2(c):
                base = c * (2 * CP - 1 + 6) + 2 * CP - 1 + 4
                dve.wait_ge(exps2_done, c + 1)
                nc.vector.tensor_reduce(row_sum2[:, :], attn2[:, :, :], AX, ALU.add).then_inc(tail_step, 1)
                dve.wait_ge(tail_step, base + 1)
                nc.vector.reciprocal(row_inv2[:, :], row_sum2[:, :]).then_inc(tail_step, 1)
                dve.wait_ge(tail_step, base + 2)
                for half in range(2):
                    rows = slice(half * N, (half + 1) * N)
                    last = tt(attn2_bd[rows, :, half * N:(half + 1) * N], attn2[rows, :, :],
                              row_inv2[rows, :].unsqueeze(2).to_broadcast([N, CP, N]), ALU.mult)
                last.then_inc(attn2_done, 1)

            def attn2_t_rest(c):
                dve.wait_ge(attn2_t_hi_done, c + 1)
                hi, lo = (s[:, :, :].rearrange("p a n -> p (a n)") for s in (attn2_t_hi, attn2_t_lo))
                tt(lo, x_ps[1][:, 0:CP * P], hi.bitcast(F32), ALU.subtract).then_inc(attn2_t_lo_done, 1)

            def t_rest(c, par, p):
                dve.wait_ge(t_hi_done, c * CP + p + 1)
                tt(t_lo[:, :], t_ps[par][p][:, :], t_hi[:, :].bitcast(F32), ALU.subtract)\
                    .then_inc(t_lo_done, 1)

            def out_elu(c, p):
                dve.wait_ge(o_exp, c * CP + p + 1)
                ts(o_buf[:, :], o_buf[:, :], 1.0, -1.0, ALU.min, ALU.add).then_inc(o_min, 1)
                dve.wait_ge(o_min, c * CP + p + 1)
                tt(o_buf[:, :], x_ps[1][:, :], o_buf[:, :], ALU.max).then_inc(o_elu, 1)

            def iteration(c, par, first, last):
                for q in range(GQ):
                    g_rest(c, q)
                for v in range(TILES):
                    dve.wait_ge(h_exp, c * TILES + v + 1)
                    full = h_full[:, v % 2, :]
                    ts(full, full, 1.0, -1.0, ALU.min, ALU.add).then_inc(h_min, 1)
                    dve.wait_ge(h_min, c * TILES + v + 1)
                    tt(full, h_ps[v % 2][:, 0:T], full, ALU.max).then_inc(h_elu, 1)
                    if first:
                        dve.wait_ge(wo_hi_done, v + 1)
                        tt(wo_lo[:, v, :], wo_raw[:, v, :], wo_hi[:, v, :].bitcast(F32), ALU.subtract)\
                            .then_inc(wo_lo_done, 1)
                    else:
                        if v < CP:
                            logits2_of(c - 1, 1 - par, v)
                        if v == 5:
                            scores2(c - 1)
                        if v == 7:
                            normalise2(c - 1)
                        if v == 10:
                            attn2_t_rest(c - 1)
                            t_rest(c - 1, 1 - par, 0)
                        if v == 12:
                            out_elu(c - 1, 0)
                            t_rest(c - 1, 1 - par, 1)
                        if v == 15:
                            out_elu(c - 1, 1)
                    if not last:
                        if v == 2:
                            logits_out(c + 1)
                        if v == 7:
                            scores(c + 1)
                        if v == 9:
                            normalise(c + 1)
                        if v == 12:
                            attn_t_rest(c + 1, 0)
                        if v == 14:
                            attn_t_rest(c + 1, 1)
                    elif v >= TILES - FT:
                        weights_rest(v - (TILES - FT))

            def weights_rest(ft):
                for k, (raw, hi, lo) in enumerate(((w1_raw, w1_hi, w1_lo), (w2_raw, w2_hi, w2_lo))):
                    dve.wait_ge(w_hi_done, 2 * ft + k + 1)
                    tt(lo[:, ft, :], raw[:, ft, :], hi[:, ft, :].bitcast(F32), ALU.subtract).then_inc(w_lo_done, 1)

            def ot_rest(c, p):
                dve.wait_ge(ot_hi_done, c * CP + p + 1)
                hi, lo = (s[:, :, p * P:(p + 1) * P] for s in (ot_hi, ot_lo))
                tt(lo, ot_ps[:, :].rearrange("p (f n) -> p f n", f=FT), hi.bitcast(F32), ALU.subtract)\
                    .then_inc(ot_lo_done, 1)

            def moments_of(c, k, source, step, ready):
                for p in range(CP):
                    dve.wait_ge(step, c * CP + p + 1)
                    nc.vector.bn_stats(stats[:, k, p, :], source[:, p, :]).then_inc(stats_done[k], 1)
                dve.wait_ge(stats_done[k], (c + 1) * CP)
                dve.sem_inc(aggr_turn, 1)
                for p in range(CP):
                    nc.vector.bn_aggr(moments[:, k, p, :], stats[:, k, p, :]).then_inc(ready, 1)

            def inverse(c, k, done):
                dve.wait_ge(done, c + 1)
                nc.vector.reciprocal(inv_std[:, k, :], std[:, k, :]).then_inc(inv_done[k], 1)
                dve.wait_ge(inv_done[k], c + 1)

            def norms(c, rest1, rest2):
                for p in range(CP):
                    dve.wait_ge(y_ps_done, c * CP + p + 1)
                    dve.wait_ge(ob_done, c * CP + p + 1)
                    tt(y[:, p, :], y_ps[p][:, :], ob[:, p, :], ALU.add).then_inc(y_done, 1)
                    if p == 0 and rest1:
                        ot_rest(c + 1, 1)
                if first_of(c):
                    out_elu(LAST, 0)
                    t_rest(LAST, LAST % 2, 1)
                moments_of(c, 0, y, y_done, mean_done)
                for p in range(CP):
                    dve.wait_ge(mean_done, c * CP + p + 1)
                    stt(z[:, p, :], y[:, p, :], moments[:, 0, p, 0:1], gamma_row[:, :], ALU.subtract,
                        ALU.mult).then_inc(scaled, 1)
                if first_of(c):
                    out_elu(LAST, 1)
                inverse(c, 0, std_done)
                for p in range(CP):
                    dve.wait_ge(xb_done, c * CP + p + 1)
                    dve.wait_ge(scaled, c * CP + p + 1)
                    stt(z[:, p, :], z[:, p, :], inv_std[:, 0, p:p + 1], xb[:, p, :], ALU.mult, ALU.add)\
                        .then_inc(z_done, 1)
                moments_of(c, 1, z, z_done, mean2_done)
                if rest2:
                    ot_rest(c + 2, 0)
                inverse(c, 1, std2_done)
                for p in range(CP):
                    after(dve, store[p], c * 16)
                    dve.wait_ge(mean2_done, c * CP + p + 1)
                    ts(res[:, p, :], z[:, p, :], moments[:, 1, p, 0:1], inv_std[:, 1, p:p + 1],
                       ALU.subtract, ALU.mult).then_inc(res_done, 1)

            def ff_iteration(c, par, first, last):
                if first:
                    scores2(LAST)
                    normalise2(LAST)
                    ot_rest(1, 0)
                    attn2_t_rest(LAST)
                    t_rest(LAST, LAST % 2, 0)
                else:
                    norms(c - 1, True, not last)

            dve.wait_ge(adj_in, 32)
            ts(limit[:, :], adj_i[:, :], 0.0, OPEN, ALU.is_gt, ALU.mult).then_inc(limit_done, 1)
            dve.wait_ge(limit_done, 1)
            ts(limit[:, :], limit[:, :], MASKED, None, ALU.add).then_inc(limit_done, 1)
            dve.wait_ge(limit_done, 2)
            dve.wait_ge(const_done, 1)
            nc.vector.memset(attn2_bd[:, :, :], 0.0)
            for i in range(HEAD_TILES):
                h, ft = i // FT, i % FT
                dve.wait_ge(wh_in[h], 16)
                dve.wait_ge(a_heads_in[h], 16)
                for j in range(2):
                    after(dve, u_done, 2 * i + j - 1)
                    nc.vector.tensor_tensor_reduce(
                        out=h_ps[j][:, :], in0=wh_raw[:, h, ft, :], in1=a_all[:, 2 * h + j, :], scale=1.0, scalar=0.0,
                        op0=ALU.mult, op1=ALU.add, accum_out=u[:, ft, j * NH + h:j * NH + h + 1])\
                        .then_inc(u_done, 1)
            logits_out(0)
            scores(0)
            normalise(0)
            attn_t_rest(0, 0)
            attn_t_rest(0, 1)
            nc.vector.memset(eps[:, :], EPS).then_inc(eps_done, 1)
            chunks(dve, iteration)
            for p in range(CP):
                ot_rest(0, p)
            for p in range(CP):
                logits2_of(LAST, LAST % 2, p)
            dve.wait_ge(row_in, 64)
            chunks(dve, ff_iteration)
            norms(LAST, False, False)

        @block.gpsimd
        def _(pool):
            tt = nc.gpsimd.tensor_tensor

            def x_rest(c, b):
                n = c * CB + b
                pool.wait_ge(x_hi_done, n + 1)
                rest = x_split[N:P, b, :]
                tt(rest, x_dup[N:P, :], rest.bitcast(F32), ALU.subtract).then_inc(x_lo_done, 1)
                pool.wait_ge(x_lo_done, n + 1)

            def diagonal(c):
                pool.wait_ge(logits_sb, c + 1)
                pool.wait_ge(logits_ps, c + 1)
                for k, part in enumerate((f2_hi, f2_lo)):
                    tt(diag[:, k, :, :, :], part.unsqueeze(3).to_broadcast([P, CP, NH, N]),
                       node_ident[:, :].unsqueeze(1).unsqueeze(1).to_broadcast([P, CP, NH, N]), ALU.mult)\
                        .then_inc(diag_done, 1)

            def diagonal2(c):
                pool.wait_ge(logits2_done, c + 1)
                after(pool, attn2_done, c)
                tt(attn2[:, :, :], logits2[:, 1, :].unsqueeze(2).to_broadcast([P, CP, N]),
                   node_ident[:, :].unsqueeze(1).to_broadcast([P, CP, N]), ALU.mult).then_inc(diag2_done, 1)

            def iteration(c, par, first, last):
                for v in range(TILES):
                    pool.wait_ge(h_hi_done, c * TILES + v + 1)
                    tt(h_lo[:, v % RING, :], h_full[:, v % 2, :], h_hi[:, v % RING, :].bitcast(F32),
                       ALU.subtract).then_inc(h_lo_done, 1)
                    if v == 1 and not first:
                        diagonal2(c - 1)
                    if not last:
                        if v in (2, 5, 8, 11):
                            pool.wait_ge(h_lo_done, c * TILES + v + 1)
                            x_rest(c + 1, v // 3)
                        if v == 3:
                            diagonal(c + 1)

            def sums(c, par, turn):
                for p in range(CP):
                    n = c * CP + p
                    pool.wait_ge(o_load[par], turn * 16)
                    after(pool, y_done, n - CP + 1)
                    tt(ob[:, p, :], o_in[:, par, p, :], b2_row[:, :], ALU.add).then_inc(ob_done, 1)
                    pool.wait_ge(x_load[par], turn * 16)
                    after(pool, z_done, n - CP + 1)
                    tt(xb[:, p, :], x_again[:, par, p, :], beta_row[:, :], ALU.add).then_inc(xb_done, 1)

            def ff_iteration(c, par, turn):
                for dt in range(DT):
                    pool.wait_ge(hid_hi_done, c * DT + dt + 1)
                    after(pool, y_ps_done, c * CP)
                    tt(hid_lo[:, dt, :], hid[:, dt % 2, :], hid_hi[:, dt, :].bitcast(F32), ALU.subtract)\
                        .then_inc(hid_lo_done, 1)
                    if first_of(c) and dt == 0:
                        diagonal2(LAST)
                sums(c, par, turn)

            in_batch = attn2_bd[:, 0, :]
            nc.gpsimd.memset(in_batch, 0.0).then_inc(const_step, 1)
            nc.gpsimd.memset(ident[:, :], 0.0).then_inc(const_step, 1)
            pool.wait_ge(const_step, 2)
            nc.gpsimd.memset(in_batch[0:N, 0:N], 1.0).then_inc(const_step, 1)
            pool.wait_ge(const_step, 3)
            nc.gpsimd.memset(in_batch[N:P, N:P], 1.0).then_inc(const_step, 1)
            pool.wait_ge(const_step, 4)
            tt(same_batch[:, :], in_batch, in_batch, ALU.mult).then_inc(const_step, 1)
            nc.gpsimd.affine_select(out=ident[:, :], in_=ident[:, :], compare_op=ALU.not_equal, fill=1.0,
                                    base=0, pattern=[[-1, P]], channel_multiplier=1)\
                .then_inc(const_step, 1)
            pool.wait_ge(const_step, 6)
            tt(node_ident[:, :], ident[:, 0:N], ident[:, N:P], ALU.add).then_inc(const_done, 1)
            pool.wait_ge(const_done, 1)
            for i in range(HEAD_TILES):
                h, ft = i // FT, i % FT
                pool.wait_ge(wh_hi_done, i + 1)
                pool.wait_ge(u_done, 2 * (i + 1))
                tt(wh_lo[:, h, ft, :], wh_raw[:, h, ft, :], wh_hi[:, h, ft, :].bitcast(F32), ALU.subtract)\
                    .then_inc(wh_lo_done, 1)
                if i == HEAD_TILES - FT - 1:
                    diagonal(0)
                    pool.wait_ge(diag_done, 2)
                if ft == FT - 1:
                    pool.wait_ge(wh_lo_done, i + 1)
                    x_rest(0, h)
            chunks(pool, iteration)
            pool.wait_ge(t_done, LAYERS_TILES)
            pool.wait_ge(row_in, 64)
            ff_iteration(0, 0, 1)
            ff_iteration(1, 1, 1)
            with pool.Fori(1, CHUNKS // 2 - 1, 1) as i:
                ff_iteration(i * 2, 0, i + 1)
                ff_iteration(i * 2 + 1, 1, i + 1)
            ff_iteration(CHUNKS - 2, 0, CHUNKS // 2)
            ff_iteration(LAST, 1, CHUNKS // 2)


_INS = ["x", "x_t", "adj", "w_heads", "a_heads", "w_out", "a_out", "w1", "b1", "w2", "b2", "gamma", "beta"]


def kernel(**inputs):
    import concourse.bacc as bacc
    from concourse import mybir
    from concourse.bass_utils import run_bass_kernel_spmd as run

    a = {k.removeprefix("L0_gnn_"): np.asarray(v) for k, v in inputs.items()}
    batches, nodes, features = a["x"].shape
    x = a["x"].reshape(batches * nodes, features)
    x_t = x.reshape(-1, 128, features // 128, 128).transpose(0, 3, 2, 1).reshape(-1, features)
    arrays = {
        "x": x, "x_t": x_t, "adj": a["adj"], "w_heads": a["W_heads"], "a_heads": a["a_heads"],
        "w_out": a["W_out"], "a_out": a["a_out"].reshape(1, -1), "w1": a["w1"],
        "b1": a["b1"].reshape(-1, 128).T, "w2": a["w2"], "b2": a["b2"].reshape(1, -1),
        "gamma": a["ln_gamma"].reshape(1, -1), "beta": a["ln_beta"].reshape(1, -1),
    }
    arrays = {f"in_{k}": np.ascontiguousarray(v) for k, v in arrays.items()}
    nc = bacc.Bacc("TRN2", target_bir_lowering=False, num_devices=1)
    args = [nc.dram_tensor(f"in_{k}", arrays[f"in_{k}"].shape, mybir.dt.from_np(arrays[f"in_{k}"].dtype),
                           kind="ExternalInput").ap() for k in _INS]
    mid = nc.dram_tensor("mid", x.shape, mybir.dt.float32, kind="Internal").ap()
    out = nc.dram_tensor("out", x.shape, mybir.dt.float32, kind="ExternalOutput").ap()
    build(nc, *args, mid, out)
    r = run(nc, [arrays], core_ids=[0])
    return r.results[0]["out"].reshape(batches, nodes, features)
```
